# Optimizing a Trainium2 kernel written in Bass

```python
import numpy as np
import jax
import jax.numpy as jnp

def _softmax(x, axis=-1):
    return jax.nn.softmax(x, axis=axis)
def _gelu(x):
    return jax.nn.gelu(x, approximate=True)
def _silu(x):
    return jax.nn.silu(x)
def _sigmoid(x):
    return jax.nn.sigmoid(x)
def _layernorm(x, axis=-1, eps=1e-5):
    m = jnp.mean(x, axis=axis, keepdims=True)
    v = jnp.var(x, axis=axis, keepdims=True)
    return (x - m) / jnp.sqrt(v + eps)
def _scatter_add(tgt, idx, src, axis=0):
    return tgt.at[idx].add(src)
def _segment_sum(src, seg, n):
    return jax.ops.segment_sum(src, seg, n)

kernel_name = 'mk_conv_seq_d2_conv_nchw64_778ff8'

def setup_inputs(seed: int = 0):
    np.random.seed(seed)
    _w = jnp.asarray
    def _rec_inputs():
        import jax
        import jax.numpy as jnp
        _gk = jax.random.key(seed)
        x = -0.0009438 + 1 * jax.random.normal(jax.random.fold_in(_gk, 1), (2, 64, 96, 96), jnp.float32)
        return x
    x = _rec_inputs()
    def _L0_conv_setup():
        import jax, jax.numpy as jnp
        import numpy as np
        B, C, IC, H, W = (2, 64, 32, 96, 96)
        key = jax.random.key(seed)
        ks = jax.random.split(key, 8)
        s_in = 1.0 / np.sqrt(C)
        s_ic = 1.0 / np.sqrt(IC)
        return {'x': jax.random.normal(ks[0], (B, C, H, W), dtype=jnp.float32), 'Wg': jax.random.uniform(ks[1], (IC, C), jnp.float32, -s_in, s_in), 'bg': jax.random.uniform(ks[2], (IC,), jnp.float32, -s_in, s_in), 'Wt': jax.random.uniform(ks[3], (IC, C), jnp.float32, -s_in, s_in), 'bt': jax.random.uniform(ks[4], (IC,), jnp.float32, -s_in, s_in), 'Wp': jax.random.uniform(ks[5], (IC, C), jnp.float32, -s_in, s_in), 'bp': jax.random.uniform(ks[6], (IC,), jnp.float32, -s_in, s_in), 'Wo': jax.random.uniform(ks[7], (C, IC), jnp.float32, -s_ic, s_ic), 'bo': jax.random.uniform(jax.random.fold_in(key, 9), (C,), jnp.float32, -s_ic, s_ic)}
    _L0_conv_all = _L0_conv_setup()
    _L0_conv_in = {k: v for k, v in _L0_conv_all.items() if k in ('Wg', 'bg', 'Wt', 'bt', 'Wp', 'bp', 'Wo', 'bo', )}
    del _L0_conv_all

    def _L1_conv_setup():
        import jax, jax.numpy as jnp
        import numpy as np
        key = jax.random.key(seed)
        ks = jax.random.split(key, 7)
        B, C, H, W = (4, 64, 64, 64)
        C8 = C // 8
        return {'x': jax.random.normal(ks[0], (B, C, H, W), dtype=jnp.float32), 'Wq': jax.random.normal(ks[1], (C8, C), dtype=jnp.float32) * 0.05, 'bq': jax.random.normal(ks[2], (C8,), dtype=jnp.float32) * 0.05, 'Wk': jax.random.normal(ks[3], (C8, C), dtype=jnp.float32) * 0.05, 'bk': jax.random.normal(ks[4], (C8,), dtype=jnp.float32) * 0.05, 'Wv': jax.random.normal(ks[5], (C, C), dtype=jnp.float32) * 0.05, 'bv': jax.random.normal(ks[6], (C,), dtype=jnp.float32) * 0.05}
    _L1_conv_all = _L1_conv_setup()
    _L1_conv_in = {k: v for k, v in _L1_conv_all.items() if k in ('Wq', 'bq', 'Wk', 'bk', 'Wv', 'bv', )}
    del _L1_conv_all

    return {
        "x": x,
        "L0_conv_Wg": _L0_conv_in["Wg"],
        "L0_conv_bg": _L0_conv_in["bg"],
        "L0_conv_Wt": _L0_conv_in["Wt"],
        "L0_conv_bt": _L0_conv_in["bt"],
        "L0_conv_Wp": _L0_conv_in["Wp"],
        "L0_conv_bp": _L0_conv_in["bp"],
        "L0_conv_Wo": _L0_conv_in["Wo"],
        "L0_conv_bo": _L0_conv_in["bo"],
        "L1_conv_Wq": _L1_conv_in["Wq"],
        "L1_conv_bq": _L1_conv_in["bq"],
        "L1_conv_Wk": _L1_conv_in["Wk"],
        "L1_conv_bk": _L1_conv_in["bk"],
        "L1_conv_Wv": _L1_conv_in["Wv"],
        "L1_conv_bv": _L1_conv_in["bv"],
    }

def reference(x, L0_conv_Wg, L0_conv_bg, L0_conv_Wt, L0_conv_bt, L0_conv_Wp, L0_conv_bp, L0_conv_Wo, L0_conv_bo, L1_conv_Wq, L1_conv_bq, L1_conv_Wk, L1_conv_bk, L1_conv_Wv, L1_conv_bv):
    import jax
    import jax.numpy as jnp
    def _L0_conv_ref(x, Wg, bg, Wt, bt, Wp, bp, Wo, bo):
        import jax, jax.numpy as jnp
        import numpy as np
        B, C, IC, H, W = (2, 64, 32, 96, 96)
        b, c, h, w = x.shape
        n = h * w
        xf = x.reshape(b, c, n)

        def proj(Wc, bc):
            return jnp.einsum('bcn,oc->bon', xf, Wc) + bc[None, :, None]
        g = proj(Wg, bg)
        theta = proj(Wt, bt)
        phi = proj(Wp, bp)
        scores = jnp.einsum('bcn,bcm->bnm', theta, phi)
        att = jax.nn.softmax(scores, axis=-1)
        y = jnp.einsum('bnm,bcm->bcn', att, g)
        o = jnp.einsum('bcn,oc->bon', y, Wo) + bo[None, :, None]
        return o.reshape(b, c, h, w) + x

    def _L1_conv_ref(x, Wq, bq, Wk, bk, Wv, bv):
        import jax, jax.numpy as jnp
        import numpy as np
        B, C, H, W = x.shape
        N = H * W
        xf = x.reshape(B, C, N)
        q = jnp.einsum('dc,bcn->bnd', Wq, xf) + bq
        k = jnp.einsum('dc,bcn->bdn', Wk, xf) + bk[:, None]
        v = jnp.einsum('dc,bcn->bdn', Wv, xf) + bv[:, None]
        attn = jnp.einsum('bnd,bdm->bnm', q, k)
        attn = jax.nn.softmax(attn, axis=-2)
        out = jnp.einsum('bcm,bnm->bcn', v, attn)
        return out.reshape(B, C, H, W) + x

    def _gn(v, G=32, eps=1e-5):
        B_, C_, H_, W_ = v.shape
        g = v.reshape(B_, G, C_ // G, H_, W_)
        m = jnp.mean(g, axis=(2, 3, 4), keepdims=True)
        s = jnp.var(g, axis=(2, 3, 4), keepdims=True)
        return ((g - m) / jnp.sqrt(s + eps)).reshape(v.shape)

    def _ln_c(v, eps=1e-6):
        m = jnp.mean(v, axis=1, keepdims=True)
        s = jnp.var(v, axis=1, keepdims=True)
        return (v - m) / jnp.sqrt(s + eps)

    def _ln_t(v, eps=1e-5):
        m = jnp.mean(v, axis=-1, keepdims=True)
        s = jnp.var(v, axis=-1, keepdims=True)
        return (v - m) / jnp.sqrt(s + eps)

    def _to_tokens(v):
        B_, C_, H_, W_ = v.shape
        return v.reshape(B_, C_, H_ * W_).transpose(0, 2, 1)
    def _from_tokens(t, like):
        B_, C_, H_, W_ = like.shape
        return t.transpose(0, 2, 1).reshape(B_, C_, H_, W_)

    x = _L0_conv_ref(x, L0_conv_Wg, L0_conv_bg, L0_conv_Wt, L0_conv_bt, L0_conv_Wp, L0_conv_bp, L0_conv_Wo, L0_conv_bo)
    x = _L1_conv_ref(x, L1_conv_Wq, L1_conv_bq, L1_conv_Wk, L1_conv_bk, L1_conv_Wv, L1_conv_bv)
    return x


_drawn_inputs = setup_inputs


def setup_inputs(seed=0):
    import zlib

    import numpy as np

    out = dict(_drawn_inputs(seed))
    spreads = {}
    factors = {'L0_conv_bt': 4.802, 'L0_conv_bp': 8.0, 'L1_conv_bq': 8.0, 'L1_conv_bk': 8.0}
    for name, (base, spread) in spreads.items():
        noise = np.random.default_rng([zlib.crc32(name.encode()), seed]).standard_normal(out[name].shape)
        drawn = base * np.exp(spread * noise) if base else spread * noise
        out[name] = jnp.asarray(drawn.astype(out[name].dtype))
    for name, factor in factors.items():
        out[name] = (out[name] * factor).astype(out[name].dtype)
    return out
```

```python
from contextlib import ExitStack

import concourse.bass as bass
from concourse import mybir

F32 = mybir.dt.float32
F32R = mybir.dt.float32r
ALU = mybir.AluOpType
ACT = mybir.ActivationFunctionType
AX = mybir.AxisListType

BANK = 512
D = 32
P3 = 3 * D

W_T, W_P, W_Q, W_K = 0, P3, 2 * P3, 3 * P3
W_G = 4 * P3
W_V = W_G + D
W_O = W_V + 64
W_BG = W_O + 4 * 64
W_BV = W_BG + D
W_BT = W_BV + 64
W_BP, W_BQ, W_BK, W_BO = W_BT + 1, W_BT + 2, W_BT + 3, W_BT + 4
W_COLS = W_BT + 5


def attention_kernel(nc, x, wpack, out):
    B, C, N = x.shape
    H = N // 2
    T = N // 128
    TH = T // 2
    CH = H // BANK
    assert C == 64 and H % BANK == 0 and N % 128 == 0

    AW = 384
    AU = H // (2 * AW)
    A_SLOTS = 4
    UW = 3 * BANK
    THIRDS = 3
    THW = N // THIRDS
    assert THW == 2 * UW
    QW = UW // 4
    B_SLOTS = 4
    PAIRS = T // 2
    NJ = N // UW
    JH = NJ // 2
    FILLS = CH
    JORDER = (1, 4, 0, 3, 2, 5)
    STEPS = 2 * NJ
    TAIL = 4
    HALF_MAIN = (0, 0, 0, 2, 1, 2, 1, 2, 1, 2, 1, 2)
    HALF_TAIL = (1, 2, 1) + (0,) * 9
    assert sum(HALF_MAIN) == 2 * FILLS - TAIL and sum(HALF_TAIL) == TAIL
    BY_DVE = (1, 5)

    ctx = ExitStack()
    with ctx:
        def sb(name, shape, dt=F32, stack=ctx):
            return stack.enter_context(nc.sbuf_tensor(name, shape, dt))

        def sem(name):
            return ctx.enter_context(nc.semaphore(name))

        w = sb("w", [128, W_COLS])
        w_half = sb("w_half", [128, 2, P3])
        ident = sb("ident", [128, 128])
        ones = sb("ones", [128, D])
        x_sb = sb("x_sb", [128, H])
        stat = sb("stat", [128, 2, 40])
        evac = sb("evac", [128, 2, BANK])
        kslot = sb("kslot", [P3, 2, 256], F32R)
        vslot = sb("vslot", [128, 2, 128])
        vw = sb("vw", [128, 4, NJ, 64])

        with ExitStack() as l0:
            th = sb("th", [P3 + 2, N], F32R, l0)
            ph = sb("ph", [P3 + 2, N], F32R, l0)
            gT = sb("gT", [128, T * D], F32, l0)
            phslot = sb("phslot", [P3 + 2, B_SLOTS, 128], F32R, l0)
            gslot = sb("gslot", [128, B_SLOTS, D], F32, l0)
            negmax = sb("negmax", [128, T], F32, l0)
            nmh = sb("nmh", [128, T], F32R, l0)
            nml = sb("nml", [128, T], F32, l0)
            nmT = sb("nmT", [T, 2, 128], F32R, l0)
            with ExitStack() as pass_a:
                psd = sb("psd", [P3, 2, H], F32R, pass_a)
                thslot = sb("thslot", [P3, A_SLOTS, 128], F32R, pass_a)
                absd = sb("absd", [128, 2, 2, AW], F32, pass_a)
                part = sb("part", [128, 2, AU], F32, pass_a)
            with ExitStack() as pass_b:
                p0 = sb("p0", [128, 4, UW], F32, pass_b)
                psum_p = sb("psum_p", [128, THW], F32, pass_b)
                rz = sb("rz", [128, 2, QW], F32, pass_b)
                yn = sb("yn", [128, 2 * THIRDS, QW], F32, pass_b)
        with ExitStack() as l1:
            qst = sb("qst", [P3, N], F32R, l1)
            with ExitStack() as build:
                kst = sb("kst", [P3, N], F32R, build)
                vT = sb("vT", [128, T * 64], F32, build)
            p1 = sb("p1", [128, 4 * NJ - 2, UW], F32, l1)

        def p1_slot(parity, tile, j):
            if tile == 0:
                return parity * NJ + j
            if j in (0, JH):
                return 2 * NJ + (j > 0)
            others = [k for k in range(NJ) if k not in (0, JH)]
            return 2 * NJ + 2 + parity * (NJ - 2) + others.index(j)

        kst_d = nc.dram_tensor("kst_d", [P3, N], F32, kind="Internal").ap()
        vT_d = nc.dram_tensor("vT_d", [128, T * 64], F32, kind="Internal").ap()

        ps = ctx.enter_context(nc.psum_tensor("ps", [128, 8, BANK], F32))

        w_in, x_in = sem("w_in"), sem("x_in")
        waited = sem("waited")
        id_zero, const_done = sem("id_zero"), sem("const_done")
        w_half_done = sem("w_half_done")
        proj_mm, proj_hi, proj_lo = sem("proj_mm"), sem("proj_hi"), sem("proj_lo")
        th_in = [sem(f"th_in{s}") for s in range(A_SLOTS)]
        s_mm, s_abs, s_max = sem("s_mm"), sem("s_abs"), sem("s_max")
        nm_tile, nm_step, nm_t, nm_copied, nm_in = sem("nm_tile"), sem("nm_step"), sem("nm_t"), sem("nm_copied"), sem("nm_in")
        slot_in = [sem(f"slot_in{s}") for s in range(B_SLOTS)]
        st_mm, p_exp, p_summed, p_used = sem("st_mm"), sem("p_exp"), sem("p_summed"), sem("p_used")
        ones_set, o_zero, sums_zero, z_mm, z_inv, y_done = sem("ones_set"), sem("o_zero"), sem("sums_zero"), sem("z_mm"), sem("z_inv"), sem("y_done")
        wo_mm, x1_done = sem("wo_mm"), sem("x1_done")
        kv_out = sem("kv_out")
        k_in = [sem(f"k_in{s}") for s in range(2)]
        v_in = [sem(f"v_in{s}") for s in range(2)]
        t_mm, t_max, t_exp = sem("t_mm"), sem("t_max"), sem("t_exp")
        m_min, m_exp, m_sum, m_inv, m_fac, vw_done = sem("m_min"), sem("m_exp"), sem("m_sum"), sem("m_inv"), sem("m_fac"), sem("vw_done")
        fill_mm, fill_copied, fill_dve, fill_pool = sem("fill_mm"), sem("fill_copied"), sem("fill_dve"), sem("fill_pool")
        result_out = sem("result_out")

        TB = 12
        jobs0 = ([("theta", h, c) for h in range(2) for c in range(CH)]
                 + [("sum", 0, c) for c in range(CH)] + [("diff", 0, c) for c in range(CH)]
                 + [("phi", h, c) for h in range(2) for c in range(CH)]
                 + [("g", h, t) for h in range(2) for t in range(0, TH, TB)])
        jobs1 = ([("q", h, c) for h in range(2) for c in range(CH)]
                 + [("k", h, c) for h in range(2) for c in range(CH)]
                 + [("v", h, t) for h in range(2) for t in range(0, TH, TB // 2)])
        JOBS = len(jobs0) + len(jobs1)
        HI_JOBS = sum(n not in "gv" for n, _, _ in jobs0 + jobs1)
        HI_JOBS0 = sum(n not in "gv" for n, _, _ in jobs0)
        stacks = {
            "theta": (th, W_T, 1, W_BT), "phi": (ph, W_P, 2, W_BP),
            "q": (qst, W_Q, 1, W_BQ), "k": (kst, W_K, 2, W_BK),
        }

        def split_target(name, h, c):
            if name in ("sum", "diff"):
                return psd[:, int(name == "diff"), c * BANK:(c + 1) * BANK], 2, W_BP if name == "sum" else None
            dst, _, lo, bias = stacks[name]
            return dst[0:P3, h * H + c * BANK:h * H + (c + 1) * BANK], lo, bias

        A_CREDIT = 2
        B_CREDIT = 2 * B_SLOTS
        A_UNITS, B_UNITS = T * AU, THIRDS * T * 2

        def unit(k):
            return ps[:, 3 * (k % 2):3 * (k % 2) + 3, :]

        def half_fills(s, main, tail):
            got = []
            if tail:
                at = 2 * FILLS - TAIL + sum(HALF_TAIL[:s])
                got += [(2, k) for k in range(at, at + HALF_TAIL[s])]
            if main:
                at = sum(HALF_MAIN[:s])
                got += [(1, k) for k in range(at, at + HALF_MAIN[s])]
            return got

        FLUSH = [(2, k) for k in range(2 * FILLS - TAIL, 2 * FILLS)] + [(1, k) for k in range(2 * FILLS)]
        ACT_FILLS = [f for f in range(FILLS) if f not in BY_DVE]

        def fill_bank(parity, f):
            return 6 + (parity + f) % 2

        def evac_slot(parity, f):
            return (parity * len(ACT_FILLS) + ACT_FILLS.index(f)) % 2

        NM, SS, EE, WW, MIN, SUM, INV, ES = 0, 6, 12, 18, 24, 25, 26, 32

        def pair_steps(eng, step):
            step(0, 0, False, False)
            step(1, 1, True, False)
            with eng.Fori(0, PAIRS // 2 - 1) as i:
                for parity in range(2):
                    step(i * 2 + (2 + parity), parity, True, True)

        def apart(eng):
            eng.sem_inc(waited, 1)

        block = ctx.enter_context(nc.Block())

        @block.sync
        def _(sp):
            def copy_words(to, of):
                return sp.dma_start(to.bitcast(F32), of.bitcast(F32))

            sp.dma_start(w[:, :], wpack).then_inc(w_in, 16)
            sp.sem_inc(p_used, B_CREDIT)
            with sp.Fori(0, B) as b:
                for h in range(2):
                    sp.dma_start(x_sb[64 * h:64 * h + 64, :], x[bass.ds(b, 1), :, h * H:(h + 1) * H]
                                 .rearrange("a c n -> (a c) n")).then_inc(x_in, 16)

                def load_theta(s, tile):
                    copy_words(thslot[:, s, :], th[0:P3, bass.ds(tile * 128, 128)]).then_inc(th_in[s], 16)

                sp.wait_ge(proj_lo, b * JOBS + len(jobs0))
                for s in range(A_SLOTS):
                    load_theta(s, s)
                with sp.Fori(0, T // A_SLOTS - 1) as i:
                    for s in range(A_SLOTS):
                        sp.wait_ge(s_mm, b * A_UNITS + i * (A_SLOTS * AU) + (s + 1) * AU)
                        load_theta(s, i * A_SLOTS + (A_SLOTS + s))
                sp.wait_ge(ones_set, b + 1)
                sp.wait_ge(nm_copied, b + 1)
                for r in range(2):
                    copy_words(th[P3 + r:P3 + r + 1, :].rearrange("a (t n) -> a t n", n=128), nmT[:, r, :]).then_inc(nm_in, 16)
                with sp.Fori(0, THIRDS) as third:
                    with sp.Fori(0, T // B_SLOTS) as i:
                        for s in range(B_SLOTS):
                            sp.wait_ge(p_used, b * B_UNITS + third * (2 * T) + i * (2 * B_SLOTS) + 2 * (s + 1))
                            copy_words(phslot[:, s, :], ph[:, bass.ds(i * (B_SLOTS * 128) + s * 128, 128)])\
                                .then_inc(slot_in[s], 16)
                            sp.dma_start(gslot[:, s, :], gT[:, bass.ds(i * (B_SLOTS * D) + s * D, D)])\
                                .then_inc(slot_in[s], 16)
                sp.wait_ge(proj_lo, b * JOBS + JOBS)
                sp.dma_start(kst_d, kst[:, :].bitcast(F32)).then_inc(kv_out, 16)
                sp.dma_start(vT_d, vT[:, :]).then_inc(kv_out, 16)
                sp.wait_ge(kv_out, b * 32 + 32)

                def load_kv(s, pair):
                    sp.dma_start(kslot[:, s, :].bitcast(F32), kst_d[:, bass.ds(pair * 256, 256)]).then_inc(k_in[s], 16)
                    sp.dma_start(vslot[:, s, :], vT_d[:, bass.ds(pair * 128, 128)]).then_inc(v_in[s], 16)

                for s in range(2):
                    load_kv(s, s)
                with sp.Fori(0, PAIRS // 2 - 1) as i:
                    for s in range(2):
                        sp.wait_ge(vw_done, b * T + i * 4 + 2 * (s + 1))
                        load_kv(s, i * 2 + (2 + s))
                sp.wait_ge(fill_dve, b * (PAIRS * len(BY_DVE)) + PAIRS * len(BY_DVE))
                sp.wait_ge(fill_pool, b * (PAIRS * len(ACT_FILLS)) + PAIRS * len(ACT_FILLS))
                for h in range(2):
                    sp.dma_start(out[bass.ds(b, 1), :, h * H:(h + 1) * H].rearrange("a c n -> (a c) n"),
                                 x_sb[64 * h:64 * h + 64, :]).then_inc(result_out, 16)
                sp.wait_ge(result_out, b * 32 + 32)
                apart(sp)

        @block.tensor
        def _(pe):
            def project(b, jobs, base):
                for k, (name, h, c) in enumerate(jobs):
                    if k >= 8:
                        pe.wait_ge(proj_lo, b * JOBS + (base + k - 7))
                    o = ps[:, k % 8, :]
                    r = slice(64 * h, 64 * h + 64)
                    if name in ("sum", "diff"):
                        mm = nc.tensor.matmul(o[0:P3, :], w_half[:, int(name == "diff"), :],
                                              x_sb[:, c * BANK:(c + 1) * BANK], start=True, stop=True)
                    elif name in stacks:
                        col = stacks[name][1]
                        mm = nc.tensor.matmul(o[0:P3, :], w[r, col:col + P3],
                                              x_sb[r, c * BANK:(c + 1) * BANK], start=True, stop=True)
                    else:
                        col, wide = (W_G, D) if name == "g" else (W_V, 64)
                        for t in range(TB * D // wide):
                            mm = nc.tensor.matmul(o[:, t * wide:(t + 1) * wide],
                                                  x_sb[r, (c + t) * 128:(c + t + 1) * 128],
                                                  w[r, col:col + wide], start=True, stop=True)
                    mm.then_inc(proj_mm, 1)

            pe.sem_inc(s_max, A_CREDIT)
            pe.wait_ge(w_half_done, 3)
            pe.wait_ge(const_done, 2)
            with pe.Fori(0, B) as b:
                pe.wait_ge(x_in, b * 32 + 32)
                project(b, jobs0, 0)
                pe.wait_ge(proj_lo, b * JOBS + len(jobs0))
                apart(pe)
                with pe.Fori(0, T // A_SLOTS) as i:
                    for s in range(A_SLOTS):
                        pe.wait_ge(th_in[s], b * (16 * T // A_SLOTS) + i * 16 + 16)
                        for u in range(AU):
                            pe.wait_ge(s_max, b * A_UNITS + i * (A_SLOTS * AU) + (s * AU + u + 1))
                            for k in range(2):
                                for half in range(2):
                                    at = (2 * u + half) * AW
                                    mm = nc.tensor.matmul(ps[:, 4 * (u % 2) + 2 * k + half, 0:AW],
                                                          thslot[:, s, :], psd[:, k, at:at + AW],
                                                          start=True, stop=True)
                            mm.then_inc(s_mm, 1)
                pe.wait_ge(nm_step, b * 2 + 2)
                nc.tensor.transpose(ps[0:T, 0, 0:128], nmh[:, :].bitcast(F32), ident[:, :])
                nc.tensor.transpose(ps[0:T, 0, 128:256], nml[:, :], ident[:, :]).then_inc(nm_t, 1)
                pe.wait_ge(nm_copied, b + 1)
                pe.wait_ge(nm_in, b * 32 + 32)
                pe.wait_ge(ones_set, b + 1)
                apart(pe)
                with pe.Fori(0, THIRDS) as third:
                    def scores(i, k):
                        if k % 2 == 0:
                            pe.wait_ge(slot_in[k // 2 % B_SLOTS],
                                       b * (32 * THIRDS * T // B_SLOTS) + third * (32 * T // B_SLOTS) + i * 32
                                       + 32 * (k // (2 * B_SLOTS) + 1))
                        for c in range(3):
                            mm = nc.tensor.matmul(unit(k)[:, c, :], phslot[:, k // 2 % B_SLOTS, :],
                                                  th[:, bass.ds(third * THW + (k % 2 * UW + c * BANK), BANK)],
                                                  start=True, stop=True)
                        mm.then_inc(st_mm, 1)

                    def products(k):
                        for g in range(4):
                            mm = nc.tensor.matmul(ps[D * g:D * g + D, 6 + k % 2, 0:QW],
                                                  gslot[:, k // 2, :], p0[:, k % 4, g * QW:(g + 1) * QW],
                                                  start=False, stop=False, skip_group_check=True)
                        mm.then_inc(p_used, 1)

                    def tiles(i, last):
                        for k in range(2 * B_SLOTS):
                            pe.wait_ge(p_exp, b * B_UNITS + third * (2 * T) + i * (2 * B_SLOTS) + (k + 1))
                            if not last or k + 2 < 2 * B_SLOTS:
                                scores(i, k + 2)
                            products(k)

                    scores(0, 0)
                    scores(0, 1)
                    pe.wait_ge(o_zero, b * THIRDS + third + 1)
                    apart(pe)
                    with pe.Fori(0, T // B_SLOTS - 1) as i:
                        tiles(i, False)
                    tiles(T // B_SLOTS - 1, True)
                    pe.wait_ge(p_summed, b * B_UNITS + third * (2 * T) + (2 * T + B_CREDIT))
                    for u in range(2):
                        for g in range(4):
                            mm = nc.tensor.matmul(ps[D * g:D * g + D, u, 0:QW], ones[:, :],
                                                  psum_p[:, u * UW + g * QW:u * UW + (g + 1) * QW],
                                                  start=True, stop=True)
                    mm.then_inc(z_mm, 1)
                    pe.wait_ge(y_done, b * THIRDS + third + 1)
                for k in range(H // QW):
                    if k >= 8:
                        pe.wait_ge(x1_done, b * (H // QW) + (k - 7))
                    for h in range(2):
                        mm = nc.tensor.matmul(ps[64 * h:64 * h + 64, k % 8, 0:QW],
                                              w[:, W_O + 64 * (k % 4):W_O + 64 * (k % 4 + 1)],
                                              yn[:, THIRDS * h + k // 4, :], start=True, stop=True)
                    mm.then_inc(wo_mm, 1)
                pe.wait_ge(x1_done, b * (H // QW) + H // QW)
                project(b, jobs1, len(jobs0))
                pe.wait_ge(proj_lo, b * JOBS + JOBS)

                def half_fill(pair, parity, hf, early):
                    f, tile = hf // 2, hf % 2
                    bank = fill_bank(parity, f)
                    if hf < 2:
                        pe.wait_ge(vw_done, b * T + pair * 2 + (tile + 1))
                    if tile == 0 and not (early and f < 2):
                        back, g = (0, f - 2) if f >= 2 else (1, f + FILLS - 2)
                        mine, by = (BY_DVE, fill_dve) if g in BY_DVE else (ACT_FILLS, fill_copied)
                        pe.wait_ge(by, b * (PAIRS * len(mine)) + pair * len(mine)
                                   + (mine.index(g) + 1 - back * len(mine)))
                    for c in range(2):
                        j = c * JH + f // 3
                        mm = nc.tensor.matmul(ps[64 * c:64 * c + 64, bank, :], vw[:, 2 * parity + tile, j, :],
                                              p1[:, p1_slot(parity, tile, j), f % 3 * BANK:(f % 3 + 1) * BANK],
                                              start=(tile == 0), stop=(tile == 1))
                    if tile == 1:
                        mm.then_inc(fill_mm, 1)

                def step(pair, parity, main, tail):
                    for s in range(STEPS):
                        if s == 0:
                            pe.wait_ge(k_in[parity], b * (8 * PAIRS) + (pair - parity) * 8 + 16)
                        if s >= 2 or main:
                            pe.wait_ge(t_exp, b * (PAIRS * STEPS) + pair * STEPS + (s - 1))
                        for c in range(3):
                            at = JORDER[s % NJ] * UW + c * BANK
                            mm = nc.tensor.matmul(ps[:, 3 * (s % 2) + c, :],
                                                  kslot[:, parity, s // NJ * 128:(s // NJ + 1) * 128],
                                                  qst[:, at:at + BANK], start=True, stop=True)
                        mm.then_inc(t_mm, 1)
                        for back, hf in half_fills(s, main, tail):
                            half_fill(pair - back, (parity + back) % 2, hf, back == 1 and not tail)

                pair_steps(pe, step)
                for back, hf in FLUSH:
                    half_fill(PAIRS - back, (PAIRS - back) % 2, hf, False)
                pe.wait_ge(fill_copied, b * (PAIRS * len(ACT_FILLS)) + PAIRS * len(ACT_FILLS))
                pe.wait_ge(fill_dve, b * (PAIRS * len(BY_DVE)) + PAIRS * len(BY_DVE))

        @block.scalar
        def _(act):
            def project_hi(b, jobs, base):
                for k, (name, h, c) in enumerate(jobs):
                    if name in "gv":
                        continue
                    dst, _, bias = split_target(name, h, c)
                    act.wait_ge(proj_mm, b * JOBS + (base + k + 1))
                    if bias is None:
                        ins = nc.scalar.activation(dst, ps[0:P3, k % 8, :], ACT.Copy)
                    else:
                        ins = nc.scalar.activation(dst, ps[0:P3, k % 8, :], ACT.Identity,
                                                   bias=w[0:P3, bias:bias + 1])
                    ins.then_inc(proj_hi, 1)

            act.wait_ge(w_in, 16)
            with act.Fori(0, B) as b:
                project_hi(b, jobs0, 0)
                with act.Fori(0, T // 2) as i:
                    for u in range(2 * AU):
                        act.wait_ge(s_mm, b * A_UNITS + i * (2 * AU) + (u + 1))
                        act.wait_ge(s_max, b * A_UNITS + i * (2 * AU) + (u + 1))
                        at = 4 * (u % 2) + 2
                        nc.scalar.activation(absd[:, u % 2], ps[:, at:at + 2, 0:AW], ACT.Abs).then_inc(s_abs, 1)
                act.wait_ge(nm_t, b + 1)
                nc.scalar.activation(nmT[:, :, :], ps[0:T, 0, 0:256].rearrange("p (r n) -> p r n", r=2), ACT.Copy)\
                    .then_inc(nm_copied, 1)
                with act.Fori(0, THIRDS * T // 2) as i:
                    for k in range(4):
                        act.wait_ge(st_mm, b * B_UNITS + i * 4 + (k + 1))
                        act.wait_ge(p_used, b * B_UNITS + i * 4 + (k + 1 + B_CREDIT - 4))
                        act.wait_ge(p_summed, b * B_UNITS + i * 4 + (k + 1 + B_CREDIT - 4))
                        nc.scalar.activation(p0[:, k, :], unit(k).rearrange("p a n -> p (a n)"), ACT.Exp).then_inc(p_exp, 1)
                project_hi(b, jobs1, len(jobs0))

                def copy_fill(pair, parity, f, early):
                    e = evac_slot(parity, f)
                    n = ACT_FILLS.index(f)
                    act.wait_ge(fill_mm, b * (PAIRS * FILLS) + pair * FILLS + (f + 1))
                    if not (early and n < 2):
                        act.wait_ge(fill_pool, b * (PAIRS * len(ACT_FILLS)) + pair * len(ACT_FILLS) + (n - 1))
                    nc.scalar.activation(evac[:, e, :], ps[:, fill_bank(parity, f), :], ACT.Copy)\
                        .then_inc(fill_copied, 1)

                def step(pair, parity, main, tail):
                    for s in range(STEPS):
                        tile, j = s // NJ, JORDER[s % NJ]
                        act.wait_ge(t_max, b * (PAIRS * STEPS) + pair * STEPS + (s + 1))
                        shared = tile == 1 and j in (0, JH)
                        if main if shared else tail:
                            act.wait_ge(fill_mm, b * (PAIRS * FILLS) + pair * FILLS
                                        + (3 * (j % JH) + 3 - (1 if shared else 2) * FILLS))
                        st = stat[:, tile, :]
                        nc.scalar.activation(p1[:, p1_slot(parity, tile, j), :],
                                             ps[:, 3 * (s % 2):3 * (s % 2) + 3, :].rearrange("p a n -> p (a n)"),
                                             ACT.Exp, bias=st[:, NM + j:NM + j + 1],
                                             accum_out=st[:, SS + j:SS + j + 1]).then_inc(t_exp, 1)
                        if s % NJ == NJ - 1:
                            act.wait_ge(m_min, b * T + pair * 2 + (tile + 1))
                            nc.scalar.activation(st[:, EE:EE + NJ], st[:, NM:NM + NJ], ACT.Exp,
                                                 bias=st[:, MIN:MIN + 1], scale=-1.0).then_inc(m_exp, 1)
                        for back, hf in half_fills(s, main, tail):
                            if hf % 2 and hf // 2 in ACT_FILLS:
                                copy_fill(pair - back, (parity + back) % 2, hf // 2, back == 1 and not tail)

                pair_steps(act, step)
                for back, hf in FLUSH:
                    if hf % 2 and hf // 2 in ACT_FILLS:
                        copy_fill(PAIRS - back, (PAIRS - back) % 2, hf // 2, False)

        @block.vector
        def _(dve):
            def project_lo(b, jobs, base, hi_base):
                his = 0
                for k, (name, h, c) in enumerate(jobs):
                    if name in "gv":
                        bias, wide, dst = (W_BG, D, gT) if name == "g" else (W_BV, 64, vT)
                        n = TB * D // wide
                        at = (h * TH + c) * wide
                        dve.wait_ge(proj_mm, b * JOBS + (base + k + 1))
                        nc.vector.tensor_tensor(
                            dst[:, at:at + n * wide].rearrange("p (t d) -> p t d", d=wide),
                            ps[:, k % 8, 0:n * wide].rearrange("p (t d) -> p t d", d=wide),
                            w[:, bias:bias + wide].unsqueeze(1).broadcast_to((128, n, wide)),
                            ALU.add).then_inc(proj_lo, 1)
                        continue
                    his += 1
                    dst, lo, bias = split_target(name, h, c)
                    r = slice(D * lo, D * lo + D)
                    dve.wait_ge(proj_hi, b * HI_JOBS + (hi_base + his))
                    if bias is None:
                        ins = nc.vector.tensor_tensor(dst[r, :], ps[r, k % 8, :], dst[r, :].bitcast(F32), ALU.subtract)
                    else:
                        ins = nc.vector.scalar_tensor_tensor(
                            out=dst[r, :], in0=ps[r, k % 8, :], scalar=w[r, bias:bias + 1],
                            in1=dst[r, :].bitcast(F32), op0=ALU.add, op1=ALU.subtract)
                    ins.then_inc(proj_lo, 1)

            dve.sem_inc(p_summed, B_CREDIT)
            dve.wait_ge(w_in, 16)
            wp = w[:, W_P:W_P + P3]
            nc.vector.tensor_scalar(w_half[:, 0, :], wp, 0.5, None, ALU.mult).then_inc(w_half_done, 1)
            nc.vector.tensor_scalar(w_half[0:64, 1, :], wp[0:64, :], 0.5, None, ALU.mult).then_inc(w_half_done, 1)
            nc.vector.tensor_scalar(w_half[64:128, 1, :], wp[64:128, :], -0.5, None, ALU.mult).then_inc(w_half_done, 1)
            with dve.Fori(0, B) as b:
                project_lo(b, jobs0, 0, 0)
                with dve.Fori(0, T // 2) as i:
                    for u in range(2 * AU):
                        dve.wait_ge(s_abs, b * A_UNITS + i * (2 * AU) + (u + 1))
                        apart(dve)
                        at = 4 * (u % 2)
                        nc.vector.tensor_tensor_reduce(
                            out=absd[:, u % 2], in0=ps[:, at:at + 2, 0:AW], in1=absd[:, u % 2], scale=1.0,
                            scalar=-3.0e38, op0=ALU.add, op1=ALU.max,
                            accum_out=part[:, u // AU, u % AU:u % AU + 1]).then_inc(s_max, 1)
                        if u % AU == AU - 1:
                            dve.wait_ge(s_max, b * A_UNITS + i * (2 * AU) + (u + 1 + A_CREDIT))
                            nc.vector.tensor_reduce(negmax[:, bass.ds(i * 2 + u // AU, 1)], part[:, u // AU, :],
                                                    AX.X, ALU.max, negate=True).then_inc(nm_tile, 1)
                dve.wait_ge(nm_tile, b * T + T)
                nc.vector.tensor_copy(nmh[:, :], negmax[:, :]).then_inc(nm_step, 1)
                dve.wait_ge(nm_step, b * 2 + 1)
                nc.vector.tensor_tensor(nml[:, :], negmax[:, :], nmh[:, :].bitcast(F32), ALU.subtract)\
                    .then_inc(nm_step, 1)
                with dve.Fori(0, THIRDS) as third:
                    nc.vector.memset(ps[:, 6:8, 0:QW], 0.0).then_inc(o_zero, 1)
                    dve.wait_ge(sums_zero, b * THIRDS + third + 1)
                    apart(dve)
                    with dve.Fori(0, T // 2) as i:
                        for k in range(4):
                            dve.wait_ge(p_exp, b * B_UNITS + third * (2 * T) + i * 4 + (k + 1))
                            dve.wait_ge(p_summed, b * B_UNITS + third * (2 * T) + i * 4 + (k - 1 + B_CREDIT))
                            sums = psum_p[:, k % 2 * UW:(k % 2 + 1) * UW]
                            nc.vector.tensor_tensor(sums, p0[:, k, :], sums, ALU.add).then_inc(p_summed, 1)
                    dve.wait_ge(z_mm, b * THIRDS + third + 1)
                    nc.vector.reciprocal(rz[:, :, :], ps[:, 0:2, 0:QW]).then_inc(z_inv, 1)
                    dve.wait_ge(z_inv, b * THIRDS + third + 1)
                    nc.vector.tensor_tensor(yn[:, bass.ds(third * 2, 2), :], ps[:, 6:8, 0:QW], rz[:, :, :], ALU.mult)\
                        .then_inc(y_done, 1)
                    dve.wait_ge(y_done, b * THIRDS + third + 1)
                for k in range(H // QW):
                    dve.wait_ge(wo_mm, b * (H // QW) + (k + 1))
                    xs = x_sb[:, k * QW:(k + 1) * QW]
                    nc.vector.scalar_tensor_tensor(out=xs, in0=ps[:, k % 8, 0:QW], scalar=w[:, W_BO:W_BO + 1],
                                                   in1=xs, op0=ALU.add, op1=ALU.add).then_inc(x1_done, 1)
                project_lo(b, jobs1, len(jobs0), HI_JOBS0)

                FIRST = BY_DVE[0]

                def add_fill(pair, parity, f, first):
                    dve.wait_ge(fill_mm, b * (PAIRS * FILLS) + pair * FILLS + (f + 1))
                    n = BY_DVE.index(f)
                    if not first:
                        dve.wait_ge(fill_dve, b * (PAIRS * len(BY_DVE)) + pair * len(BY_DVE) + n)
                    xs = x_sb[:, f * BANK:(f + 1) * BANK]
                    nc.vector.tensor_tensor(xs, ps[:, fill_bank(parity, f), :], xs, ALU.add).then_inc(fill_dve, 1)

                def factors(pair, tile, early):
                    st = stat[:, tile, :]
                    dve.wait_ge(m_exp, b * T + pair * 2 + (tile + 1))
                    nc.vector.tensor_tensor_reduce(out=st[:, ES:ES + NJ], in0=st[:, EE:EE + NJ], in1=st[:, SS:SS + NJ],
                                                   scale=1.0, scalar=0.0, op0=ALU.mult, op1=ALU.add,
                                                   accum_out=st[:, SUM:SUM + 1]).then_inc(m_sum, 1)
                    dve.wait_ge(m_sum, b * T + pair * 2 + (tile + 1))
                    nc.vector.reciprocal(st[:, INV:INV + 1], st[:, SUM:SUM + 1]).then_inc(m_inv, 1)
                    dve.wait_ge(m_inv, b * T + pair * 2 + (tile + 1))
                    if not early:
                        dve.wait_ge(vw_done, b * T + pair * 2 + (tile - 1))
                    nc.vector.tensor_scalar(st[:, WW:WW + NJ], st[:, EE:EE + NJ], st[:, INV:INV + 1], None, ALU.mult)\
                        .then_inc(m_fac, 1)

                def step(pair, parity, main, tail):
                    for s in range(STEPS):
                        tile, j = s // NJ, JORDER[s % NJ]
                        st = stat[:, tile, :]
                        dve.wait_ge(t_mm, b * (PAIRS * STEPS) + pair * STEPS + (s + 1))
                        nc.vector.tensor_reduce(st[:, NM + j:NM + j + 1], ps[:, 3 * (s % 2):3 * (s % 2) + 3, :]
                                                .rearrange("p a n -> p (a n)"), AX.X, ALU.max, negate=True)\
                            .then_inc(t_max, 1)
                        if s % NJ == NJ - 1:
                            dve.wait_ge(t_max, b * (PAIRS * STEPS) + pair * STEPS + (s + 1))
                            nc.vector.tensor_reduce(st[:, MIN:MIN + 1], st[:, NM:NM + NJ], AX.X, ALU.min)\
                                .then_inc(m_min, 1)
                        if s == 0 and main:
                            factors(pair - 1, 1, not tail)
                        if s == NJ:
                            factors(pair, 0, not main)
                        for back, hf in half_fills(s, main, tail):
                            if hf % 2 and hf // 2 in BY_DVE:
                                add_fill(pair - back, (parity + back) % 2, hf // 2, not tail and hf // 2 == FIRST)

                pair_steps(dve, step)
                factors(PAIRS - 1, 1, False)
                for back, hf in FLUSH:
                    if hf % 2 and hf // 2 in BY_DVE:
                        add_fill(PAIRS - back, (PAIRS - back) % 2, hf // 2, False)

        @block.gpsimd
        def _(pool):
            nc.gpsimd.memset(ident[:, :], 0.0).then_inc(id_zero, 1)
            pool.wait_ge(id_zero, 1)
            nc.gpsimd.affine_select(out=ident[:, :], in_=ident[:, :], compare_op=ALU.not_equal, fill=1.0, base=0,
                                    pattern=[[-1, 128]], channel_multiplier=1).then_inc(const_done, 1)
            nc.gpsimd.memset(ones[:, :], 1.0).then_inc(const_done, 1)
            pool.wait_ge(const_done, 2)
            with pool.Fori(0, B) as b:
                nc.gpsimd.memset(ph[P3:P3 + 2, :].bitcast(F32), 1.0).then_inc(ones_set, 1)
                pool.wait_ge(ones_set, b + 1)
                pool.wait_ge(nm_in, b * 32 + 32)
                apart(pool)
                with pool.Fori(0, THIRDS) as third:
                    nc.gpsimd.memset(psum_p[:, :], 0.0).then_inc(sums_zero, 1)
                    pool.wait_ge(z_mm, b * THIRDS + third + 1)

                FIRST = ACT_FILLS[0]

                def add_fill(pair, parity, f, first):
                    n = ACT_FILLS.index(f)
                    count = b * (PAIRS * len(ACT_FILLS)) + pair * len(ACT_FILLS) + (n + 1)
                    pool.wait_ge(fill_copied, count)
                    if not first:
                        pool.wait_ge(fill_pool, count - 1)
                    xs = x_sb[:, f * BANK:(f + 1) * BANK]
                    nc.gpsimd.tensor_tensor(xs, evac[:, evac_slot(parity, f), :], xs, ALU.add).then_inc(fill_pool, 1)

                def weigh_v(pair, parity, tile):
                    pool.wait_ge(m_fac, b * T + pair * 2 + (tile + 1))
                    pool.wait_ge(v_in[parity], b * (8 * PAIRS) + (pair - parity) * 8 + 16)
                    nc.gpsimd.tensor_tensor(
                        vw[:, 2 * parity + tile],
                        vslot[:, parity, 64 * tile:64 * tile + 64].unsqueeze(1).broadcast_to((128, NJ, 64)),
                        stat[:, tile, WW:WW + NJ].unsqueeze(2).broadcast_to((128, NJ, 64)),
                        ALU.mult).then_inc(vw_done, 1)

                def step(pair, parity, main, tail):
                    for s in range(STEPS):
                        if s == 0 and main:
                            weigh_v(pair - 1, 1 - parity, 1)
                        if s == NJ:
                            weigh_v(pair, parity, 0)
                        for back, hf in half_fills(s, main, tail):
                            if hf % 2 and hf // 2 in ACT_FILLS:
                                add_fill(pair - back, (parity + back) % 2, hf // 2, not tail and hf // 2 == FIRST)

                pair_steps(pool, step)
                weigh_v(PAIRS - 1, (PAIRS - 1) % 2, 1)
                for back, hf in FLUSH:
                    if hf % 2 and hf // 2 in ACT_FILLS:
                        add_fill(PAIRS - back, (PAIRS - back) % 2, hf // 2, False)
                pool.wait_ge(fill_pool, b * (PAIRS * len(ACT_FILLS)) + PAIRS * len(ACT_FILLS))
                apart(pool)


def pack_weights(Wg, bg, Wt, bt, Wp, bp, Wo, bo, Wq, bq, Wk, bk, Wv, bv):
    import numpy as np

    pack = np.zeros((128, W_COLS), np.float32)

    def stack(col, bias_col, W, b):
        for block in range(3):
            for half in range(2):
                pack[64 * half:64 * half + 64, col + D * block:col + D * block + W.shape[0]] = W.T
            pack[D * block:D * block + W.shape[0], bias_col] = b

    stack(W_T, W_BT, Wt, bt)
    stack(W_P, W_BP, Wp, bp)
    stack(W_Q, W_BQ, Wq, bq)
    stack(W_K, W_BK, Wk, bk)
    for half in range(2):
        rows = slice(64 * half, 64 * half + 64)
        pack[rows, W_G:W_G + D] = Wg.T
        pack[rows, W_V:W_V + 64] = Wv.T
        pack[rows, W_BO] = bo
    for group in range(4):
        pack[D * group:D * group + D, W_O + 64 * group:W_O + 64 * group + 64] = Wo.T
    pack[:, W_BG:W_BG + D] = bg
    pack[:, W_BV:W_BV + 64] = bv
    return pack


def kernel(**inputs):
    import numpy as np
    import concourse.bacc as bacc
    from concourse.bass_utils import run_bass_kernel_spmd

    a = {k: np.asarray(v) for k, v in inputs.items()}
    B, C, HH, WWD = a["x"].shape
    arrays = {
        "x": np.ascontiguousarray(a["x"]).reshape(B, C, HH * WWD),
        "wpack": pack_weights(*[a[f"L0_conv_{n}"] for n in ("Wg", "bg", "Wt", "bt", "Wp", "bp", "Wo", "bo")],
                              *[a[f"L1_conv_{n}"] for n in ("Wq", "bq", "Wk", "bk", "Wv", "bv")]),
    }
    nc = bacc.Bacc("TRN2", target_bir_lowering=False, num_devices=1)
    aps = [nc.dram_tensor(n, v.shape, mybir.dt.from_np(v.dtype), kind="ExternalInput").ap() for n, v in arrays.items()]
    out = nc.dram_tensor("out", (B, C, HH * WWD), F32, kind="ExternalOutput").ap()
    attention_kernel(nc, *aps, out)
    r = run_bass_kernel_spmd(nc, [arrays], core_ids=[0])
    return r.results[0]["out"].reshape(B, C, HH, WWD)
```

```python
from contextlib import ExitStack

import concourse.bass as bass
from concourse import mybir

F32 = mybir.dt.float32
F32R = mybir.dt.float32r
ALU = mybir.AluOpType
ACT = mybir.ActivationFunctionType
AX = mybir.AxisListType

BANK = 512
D = 32
P3 = 3 * D
K = 128

W_T, W_P, W_Q, W_K = 0, 2 * P3, 4 * P3, 6 * P3
W_G = 8 * P3
W_V = W_G + D
W_O = W_V + 64
W_BG = W_O + 4 * 64
W_BV = W_BG + D
W_BT = W_BV + 64
W_BP, W_BQ, W_BK, W_BO = W_BT + 1, W_BT + 2, W_BT + 3, W_BT + 4
W_COLS = W_BT + 5


def attention_kernel(nc, x, wpack, out):
    B, C, N = x.shape
    H = N // 2
    T = N // 128
    TH = T // 2
    CH = H // BANK
    assert C == 64 and H % BANK == 0 and N % 128 == 0

    PARTS = 3
    PW = H // PARTS

    AW = 384
    AU = H // (2 * AW)
    A_SLOTS = 4
    UW = 3 * BANK
    THIRDS = 3
    THW = N // THIRDS
    assert THW == 2 * UW
    QW = UW // 4
    QD = 320
    B_SLOTS = 4
    PAIRS = T // 2
    JW = 2 * BANK
    NJ = N // JW
    FILLS = CH
    STEPS = 2 * NJ
    assert STEPS == 2 * FILLS and STEPS % 3 == 0
    LAG = 3

    def chunk_of(c, f):
        return (c * CH + f) // 2, (c * CH + f) % 2

    LAST_FILL = [max(f for c in range(2) for f in range(FILLS) if chunk_of(c, f)[0] == j) for j in range(NJ)]
    BY_USE = sorted(range(NJ), key=lambda j: LAST_FILL[j])
    SHARED = BY_USE[:4]
    ORDER = [(0, j) for j in BY_USE] + [(1, j) for j in BY_USE[4:] + SHARED]
    assert all(2 * LAST_FILL[j] + 1 + LAG < STEPS - len(SHARED) for j in SHARED)
    BY_DVE = (1, 5)

    ctx = ExitStack()
    with ctx:
        def sb(name, shape, dt=F32, stack=ctx):
            return stack.enter_context(nc.sbuf_tensor(name, shape, dt))

        def sem(name):
            return ctx.enter_context(nc.semaphore(name))

        w = sb("w", [128, W_COLS])
        w_half = sb("w_half", [128, 2, P3])
        ident = sb("ident", [128, 128])
        ones = sb("ones", [128, D])
        x_sb = sb("x_sb", [128, H])
        stat = sb("stat", [128, 2, 54])
        evac = sb("evac", [128, 2, BANK])
        kslot = sb("kslot", [K, 2, 256], F32R)
        vslot = sb("vslot", [128, 2, 128])
        vw = sb("vw", [128, 4, NJ, 64])

        with ExitStack() as l0:
            th = sb("th", [K, N], F32R, l0)
            ph = sb("ph", [K, N], F32R, l0)
            gT = sb("gT", [128, T * D], F32, l0)
            phslot = sb("phslot", [K, B_SLOTS, 128], F32R, l0)
            gslot = sb("gslot", [128, B_SLOTS, D], F32, l0)
            negmax = sb("negmax", [128, T], F32, l0)
            nmh = sb("nmh", [128, T], F32R, l0)
            nml = sb("nml", [128, T], F32, l0)
            nmT = sb("nmT", [T, 2, 128], F32R, l0)
            with ExitStack() as pass_a:
                psd = sb("psd", [K, 2, H], F32R, pass_a)
                thslot = sb("thslot", [K, A_SLOTS, 128], F32R, pass_a)
                absd = sb("absd", [128, 3, 2, AW], F32, pass_a)
                part = sb("part", [128, 2, AU], F32, pass_a)
            with ExitStack() as pass_b:
                p0 = sb("p0", [128, 4, UW], F32, pass_b)
                psum_p = sb("psum_p", [128, 2, 4, QD], F32, pass_b)
                z_sb = sb("z_sb", [128, 2, QW], F32, pass_b)
                yn = sb("yn", [128, 2 * THIRDS, QW], F32, pass_b)
        with ExitStack() as l1:
            qst = sb("qst", [K, N], F32R, l1)
            with ExitStack() as build:
                kst = sb("kst", [P3, N], F32R, build)
                vT = sb("vT", [128, T * 64], F32, build)
            p1 = sb("p1", [128, 4 * NJ - len(SHARED), JW], F32, l1)

        def p1_slot(parity, tile, j):
            if tile == 0:
                return parity * NJ + j
            if j in SHARED:
                return 2 * NJ + SHARED.index(j)
            return 2 * NJ + len(SHARED) + parity * (NJ - len(SHARED)) + BY_USE[len(SHARED):].index(j)

        kst_d = nc.dram_tensor("kst_d", [P3, N], F32, kind="Internal").ap()
        vT_d = nc.dram_tensor("vT_d", [128, T * 64], F32, kind="Internal").ap()

        ps = ctx.enter_context(nc.psum_tensor("ps", [128, 8, BANK], F32))

        w_in, x_in = sem("w_in"), [sem(f"x_in{k}") for k in range(PARTS)]
        waited = sem("waited")
        id_zero, const_done = sem("id_zero"), sem("const_done")
        w_half_done = sem("w_half_done")
        proj_mm, proj_hi, proj_lo = sem("proj_mm"), sem("proj_hi"), sem("proj_lo")
        th_in = [sem(f"th_in{s}") for s in range(A_SLOTS)]
        d_mm, s_mm, s_abs, s_max = sem("d_mm"), sem("s_mm"), sem("s_abs"), sem("s_max")
        nm_tile, nm_step, nm_t, nm_copied, nm_in = sem("nm_tile"), sem("nm_step"), sem("nm_t"), sem("nm_copied"), sem("nm_in")
        slot_in = [sem(f"slot_in{s}") for s in range(B_SLOTS)]
        st_mm, p_exp, p_summed, p_used = sem("st_mm"), sem("p_exp"), sem("p_summed"), sem("p_used")
        rest_zero, ones_set, q_zero, o_zero, sums_zero, z_mm, z_copied, z_rest, z_inv, y_done = sem("rest_zero"), sem("ones_set"), sem("q_zero"), sem("o_zero"), sem("sums_zero"), sem("z_mm"), sem("z_copied"), sem("z_rest"), sem("z_inv"), sem("y_done")
        wo_mm, x1_done = sem("wo_mm"), sem("x1_done")
        kv_out = sem("kv_out")
        k_in = [sem(f"k_in{s}") for s in range(2)]
        v_in = [sem(f"v_in{s}") for s in range(2)]
        t_mm, t_max, t_exp = sem("t_mm"), sem("t_max"), sem("t_exp")
        m_min, m_exp, m_sum, m_inv, m_fac, vw_done = sem("m_min"), sem("m_exp"), sem("m_sum"), sem("m_inv"), sem("m_fac"), sem("vw_done")
        fill_mm, fill_copied, fill_dve, fill_pool = sem("fill_mm"), sem("fill_copied"), sem("fill_dve"), sem("fill_pool")
        result_out = sem("result_out")

        TB = 12
        jobs0 = ([("theta", h, c) for c in range(CH) for h in range(2)]
                 + [("sum", 0, c) for c in range(CH)] + [("diff", 0, c) for c in range(CH)]
                 + [("phi", h, c) for h in range(2) for c in range(CH)]
                 + [("g", h, t) for h in range(2) for t in range(0, TH, TB)])
        jobs1 = ([("q", h, c) for h in range(2) for c in range(CH)]
                 + [("k", h, c) for h in range(2) for c in range(CH)]
                 + [("v", h, t) for h in range(2) for t in range(0, TH, TB // 2)])
        JOBS = len(jobs0) + len(jobs1)
        HI_JOBS = sum(n not in "gv" for n, _, _ in jobs0 + jobs1)
        HI_JOBS0 = sum(n not in "gv" for n, _, _ in jobs0)
        stacks = {
            "theta": (th, W_T, 1, W_BT), "phi": (ph, W_P, 2, W_BP),
            "q": (qst, W_Q, 1, W_BQ), "k": (kst, W_K, 2, W_BK),
        }

        def split_target(name, h, c):
            if name in ("sum", "diff"):
                return psd[0:P3, int(name == "diff"), c * BANK:(c + 1) * BANK], 2, W_BP if name == "sum" else None
            dst, _, lo, bias = stacks[name]
            return dst[0:P3, h * H + c * BANK:h * H + (c + 1) * BANK], lo, bias

        A_CREDIT = 3
        B_CREDIT = 2 * B_SLOTS
        A_UNITS, B_UNITS = T * AU, THIRDS * T * 2

        def unit(k):
            return ps[:, 3 * (k % 2):3 * (k % 2) + 3, :]

        def half_fills(s, main, tail):
            if s < LAG:
                return [(2, STEPS - LAG + s)] if tail else []
            return [(1, s - LAG)] if main else []

        FLUSH = [(2, k) for k in range(STEPS - LAG, STEPS)] + [(1, k) for k in range(STEPS)]
        ACT_FILLS = [f for f in range(FILLS) if f not in BY_DVE]

        def chunk_scores(s):
            return ps[:, 2 * (s % 3):2 * (s % 3) + 2, :]

        def fill_bank(parity, f):
            return 6 + (parity + f) % 2

        def evac_slot(parity, f):
            return (parity * len(ACT_FILLS) + ACT_FILLS.index(f)) % 2

        NM, SS, EE, WW, ES, MIN, SUM, INV = 0, 10, 20, 30, 40, 50, 51, 52

        def pair_steps(eng, step):
            step(0, 0, False, False)
            step(1, 1, True, False)
            with eng.Fori(0, PAIRS // 2 - 1) as i:
                for parity in range(2):
                    step(i * 2 + (2 + parity), parity, True, True)

        def apart(eng):
            eng.sem_inc(waited, 1)

        block = ctx.enter_context(nc.Block())

        @block.sync
        def _(sp):
            def copy_words(to, of):
                return sp.dma_start(to.bitcast(F32), of.bitcast(F32))

            sp.dma_start(w[:, :], wpack).then_inc(w_in, 16)
            sp.sem_inc(p_used, B_CREDIT)
            with sp.Fori(0, B) as b:
                for k in range(PARTS):
                    for h in range(2):
                        sp.dma_start(x_sb[64 * h:64 * h + 64, k * PW:(k + 1) * PW],
                                     x[bass.ds(b, 1), :, h * H + k * PW:h * H + (k + 1) * PW]
                                     .rearrange("a c n -> (a c) n")).then_inc(x_in[k], 16)

                def load_theta(s, tile):
                    copy_words(thslot[0:P3, s, :], th[0:P3, bass.ds(tile * 128, 128)]).then_inc(th_in[s], 16)

                sp.wait_ge(proj_lo, b * JOBS + len(jobs0))
                for s in range(A_SLOTS):
                    load_theta(s, s)
                with sp.Fori(0, T // A_SLOTS - 1) as i:
                    for s in range(A_SLOTS):
                        sp.wait_ge(s_mm, b * A_UNITS + i * (A_SLOTS * AU) + (s + 1) * AU)
                        load_theta(s, i * A_SLOTS + (A_SLOTS + s))
                sp.wait_ge(ones_set, b + 1)
                sp.wait_ge(nm_copied, b + 1)
                for r in range(2):
                    copy_words(th[P3 + r:P3 + r + 1, :].rearrange("a (t n) -> a t n", n=128), nmT[:, r, :]).then_inc(nm_in, 16)
                with sp.Fori(0, THIRDS) as third:
                    with sp.Fori(0, T // B_SLOTS) as i:
                        for s in range(B_SLOTS):
                            sp.wait_ge(p_used, b * B_UNITS + third * (2 * T) + i * (2 * B_SLOTS) + 2 * (s + 1))
                            copy_words(phslot[:, s, :], ph[:, bass.ds(i * (B_SLOTS * 128) + s * 128, 128)])\
                                .then_inc(slot_in[s], 16)
                            sp.dma_start(gslot[:, s, :], gT[:, bass.ds(i * (B_SLOTS * D) + s * D, D)])\
                                .then_inc(slot_in[s], 16)
                sp.wait_ge(proj_lo, b * JOBS + JOBS)
                sp.dma_start(kst_d, kst[:, :].bitcast(F32)).then_inc(kv_out, 16)
                sp.dma_start(vT_d, vT[:, :]).then_inc(kv_out, 16)
                sp.wait_ge(kv_out, b * 32 + 32)

                def load_kv(s, pair):
                    sp.dma_start(kslot[0:P3, s, :].bitcast(F32), kst_d[:, bass.ds(pair * 256, 256)]).then_inc(k_in[s], 16)
                    sp.dma_start(vslot[:, s, :], vT_d[:, bass.ds(pair * 128, 128)]).then_inc(v_in[s], 16)

                for s in range(2):
                    load_kv(s, s)
                with sp.Fori(0, PAIRS // 2 - 1) as i:
                    for s in range(2):
                        sp.wait_ge(vw_done, b * T + i * 4 + 2 * (s + 1))
                        load_kv(s, i * 2 + (2 + s))
                for k in range(PARTS):
                    done = (k + 1) * FILLS // PARTS
                    last = (PAIRS - 1, [f for f in BY_DVE if f < done], [f for f in ACT_FILLS if f < done])
                    sp.wait_ge(fill_dve, b * (PAIRS * len(BY_DVE)) + last[0] * len(BY_DVE) + len(last[1]))
                    apart(sp)
                    sp.wait_ge(fill_pool, b * (PAIRS * len(ACT_FILLS)) + last[0] * len(ACT_FILLS) + len(last[2]))
                    for h in range(2):
                        sp.dma_start(out[bass.ds(b, 1), :, h * H + k * PW:h * H + (k + 1) * PW]
                                     .rearrange("a c n -> (a c) n"),
                                     x_sb[64 * h:64 * h + 64, k * PW:(k + 1) * PW]).then_inc(result_out, 16)
                sp.wait_ge(result_out, b * (32 * PARTS) + 32 * PARTS)
                apart(sp)

        @block.tensor
        def _(pe):
            def project(b, jobs, base):
                for k, (name, h, c) in enumerate(jobs):
                    if k >= 8:
                        pe.wait_ge(proj_lo, b * JOBS + (base + k - 7))
                    if base == 0 and k % (2 * CH // PARTS) == 0 and k < 2 * CH:
                        pe.wait_ge(x_in[k // (2 * CH // PARTS)], b * 32 + 32)
                    o = ps[:, k % 8, :]
                    r = slice(64 * h, 64 * h + 64)
                    if name in ("sum", "diff"):
                        mm = nc.tensor.matmul(o[0:P3, :], w_half[:, int(name == "diff"), :],
                                              x_sb[:, c * BANK:(c + 1) * BANK], start=True, stop=True)
                    elif name in stacks:
                        col = stacks[name][1]
                        mm = nc.tensor.matmul(o[0:P3, :], w[:, col + h * P3:col + (h + 1) * P3],
                                              x_sb[:, c * BANK:(c + 1) * BANK], start=True, stop=True)
                    else:
                        col, wide = (W_G, D) if name == "g" else (W_V, 64)
                        for t in range(TB * D // wide):
                            mm = nc.tensor.matmul(o[:, t * wide:(t + 1) * wide],
                                                  x_sb[r, (c + t) * 128:(c + t + 1) * 128],
                                                  w[r, col:col + wide], start=True, stop=True)
                    mm.then_inc(proj_mm, 1)

            pe.sem_inc(s_max, A_CREDIT)
            pe.sem_inc(s_abs, A_CREDIT)
            pe.wait_ge(w_half_done, 4)
            pe.wait_ge(const_done, 3)
            with pe.Fori(0, B) as b:
                project(b, jobs0, 0)
                pe.wait_ge(proj_lo, b * JOBS + len(jobs0))
                pe.wait_ge(rest_zero, b * 4 + 4)
                apart(pe)
                with pe.Fori(0, T // A_SLOTS) as i:
                    for s in range(A_SLOTS):
                        pe.wait_ge(th_in[s], b * (16 * T // A_SLOTS) + i * 16 + 16)
                        at = b * A_UNITS + i * (A_SLOTS * AU) + s * AU

                        def half_unit(k, u):
                            for half in range(2):
                                col = (2 * u + half) * AW
                                mm = nc.tensor.matmul(ps[:, 4 * (u % 2) + 2 * k + half, 0:AW], thslot[:, s, :],
                                                      psd[:, k, col:col + AW], start=True, stop=True)
                            mm.then_inc(d_mm if k else s_mm, 1)

                        for u in range(AU + 1):
                            if u < AU:
                                pe.wait_ge(s_abs, at + (u + A_CREDIT - 1))
                                half_unit(1, u)
                            if u >= 1:
                                pe.wait_ge(s_max, at + (u - 1 + A_CREDIT - 1))
                                half_unit(0, u - 1)
                pe.wait_ge(nm_step, b * 2 + 2)
                nc.tensor.transpose(ps[0:T, 0, 0:128], nmh[:, :].bitcast(F32), ident[:, :])
                nc.tensor.transpose(ps[0:T, 0, 128:256], nml[:, :], ident[:, :]).then_inc(nm_t, 1)
                pe.wait_ge(nm_copied, b + 1)
                pe.wait_ge(nm_in, b * 32 + 32)
                pe.wait_ge(ones_set, b + 1)
                apart(pe)
                with pe.Fori(0, THIRDS) as third:
                    def scores(i, k):
                        if k % 2 == 0:
                            pe.wait_ge(slot_in[k // 2 % B_SLOTS],
                                       b * (32 * THIRDS * T // B_SLOTS) + third * (32 * T // B_SLOTS) + i * 32
                                       + 32 * (k // (2 * B_SLOTS) + 1))
                        for c in range(3):
                            mm = nc.tensor.matmul(unit(k)[:, c, :], phslot[:, k // 2 % B_SLOTS, :],
                                                  th[:, bass.ds(third * THW + (k % 2 * UW + c * BANK), BANK)],
                                                  start=True, stop=True)
                        mm.then_inc(st_mm, 1)

                    def products(k):
                        for g in range(4):
                            nc.tensor.matmul(ps[D * g:D * g + D, 6 + k % 2, 0:QW],
                                             gslot[:, k // 2, :], p0[:, k % 4, g * QW:(g + 1) * QW],
                                             start=False, stop=False, skip_group_check=True)
                        for g in range(4):
                            mm = nc.tensor.matmul(ps[D * g:D * g + D, 6 + k % 2, QW:2 * QW - QD],
                                                  ones[:, :], p0[:, k % 4, g * QW + QD:(g + 1) * QW],
                                                  start=False, stop=False, skip_group_check=True)
                        mm.then_inc(p_used, 1)

                    def tiles(i, last):
                        for k in range(2 * B_SLOTS):
                            pe.wait_ge(p_exp, b * B_UNITS + third * (2 * T) + i * (2 * B_SLOTS) + (k + 1))
                            if not last or k + 2 < 2 * B_SLOTS:
                                scores(i, k + 2)
                            products(k)

                    scores(0, 0)
                    scores(0, 1)
                    pe.wait_ge(o_zero, b * THIRDS + third + 1)
                    apart(pe)
                    with pe.Fori(0, T // B_SLOTS - 1) as i:
                        tiles(i, False)
                    tiles(T // B_SLOTS - 1, True)
                    pe.wait_ge(p_summed, b * B_UNITS + third * (2 * T) + (2 * T + B_CREDIT))
                    for u in range(2):
                        for g in range(4):
                            mm = nc.tensor.matmul(ps[D * g:D * g + D, u, 0:QD], ones[:, :],
                                                  psum_p[:, u, g, :], start=True, stop=True)
                    mm.then_inc(z_mm, 1)
                    pe.wait_ge(z_copied, b * THIRDS + third + 1)
                    apart(pe)
                pe.wait_ge(y_done, b * THIRDS + THIRDS)
                for k in range(H // QW):
                    if k >= 8:
                        pe.wait_ge(x1_done, b * (H // QW) + (k - 7))
                    for h in range(2):
                        mm = nc.tensor.matmul(ps[64 * h:64 * h + 64, k % 8, 0:QW],
                                              w[:, W_O + 64 * (k % 4):W_O + 64 * (k % 4 + 1)],
                                              yn[:, THIRDS * h + k // 4, :], start=True, stop=True)
                    mm.then_inc(wo_mm, 1)
                pe.wait_ge(x1_done, b * (H // QW) + H // QW)
                project(b, jobs1, len(jobs0))
                pe.wait_ge(proj_lo, b * JOBS + JOBS)
                pe.wait_ge(q_zero, b + 1)

                def half_fill(pair, parity, hf, early):
                    f, tile = hf // 2, hf % 2
                    bank = fill_bank(parity, f)
                    if hf < 2:
                        pe.wait_ge(vw_done, b * T + pair * 2 + (tile + 1))
                    if tile == 0 and not (early and f < 2):
                        back, g = (0, f - 2) if f >= 2 else (1, f + FILLS - 2)
                        mine, by = (BY_DVE, fill_dve) if g in BY_DVE else (ACT_FILLS, fill_copied)
                        pe.wait_ge(by, b * (PAIRS * len(mine)) + pair * len(mine)
                                   + (mine.index(g) + 1 - back * len(mine)))
                    for c in range(2):
                        j, part = chunk_of(c, f)
                        mm = nc.tensor.matmul(ps[64 * c:64 * c + 64, bank, :], vw[:, 2 * parity + tile, j, :],
                                              p1[:, p1_slot(parity, tile, j), part * BANK:(part + 1) * BANK],
                                              start=(tile == 0), stop=(tile == 1))
                    if tile == 1:
                        mm.then_inc(fill_mm, 1)

                def step(pair, parity, main, tail):
                    for s in range(STEPS):
                        if s == 0:
                            pe.wait_ge(k_in[parity], b * (8 * PAIRS) + (pair - parity) * 8 + 16)
                        if s >= 3 or main:
                            pe.wait_ge(t_exp, b * (PAIRS * STEPS) + pair * STEPS + (s - 2))
                        tile, j = ORDER[s]
                        for c in range(2):
                            at = j * JW + c * BANK
                            mm = nc.tensor.matmul(chunk_scores(s)[:, c, :],
                                                  kslot[:, parity, tile * 128:(tile + 1) * 128],
                                                  qst[:, at:at + BANK], start=True, stop=True)
                        mm.then_inc(t_mm, 1)
                        for back, hf in half_fills(s, main, tail):
                            half_fill(pair - back, (parity + back) % 2, hf, back == 1 and not tail)

                pair_steps(pe, step)
                for back, hf in FLUSH:
                    half_fill(PAIRS - back, (PAIRS - back) % 2, hf, False)
                pe.wait_ge(fill_copied, b * (PAIRS * len(ACT_FILLS)) + PAIRS * len(ACT_FILLS))
                pe.wait_ge(fill_dve, b * (PAIRS * len(BY_DVE)) + PAIRS * len(BY_DVE))

        @block.scalar
        def _(act):
            def project_hi(b, jobs, base):
                for k, (name, h, c) in enumerate(jobs):
                    if name in "gv":
                        continue
                    dst, _, bias = split_target(name, h, c)
                    act.wait_ge(proj_mm, b * JOBS + (base + k + 1))
                    if bias is None:
                        ins = nc.scalar.activation(dst, ps[0:P3, k % 8, :], ACT.Copy)
                    else:
                        ins = nc.scalar.activation(dst, ps[0:P3, k % 8, :], ACT.Identity,
                                                   bias=w[0:P3, bias:bias + 1])
                    ins.then_inc(proj_hi, 1)

            act.wait_ge(w_in, 16)
            with act.Fori(0, B) as b:
                project_hi(b, jobs0, 0)
                with act.Fori(0, T // 2) as i:
                    for u in range(2 * AU):
                        act.wait_ge(d_mm, b * A_UNITS + i * (2 * AU) + (u + 1))
                        act.wait_ge(s_max, b * A_UNITS + i * (2 * AU) + (u + A_CREDIT - 2))
                        at = 4 * (u % 2) + 2
                        nc.scalar.activation(absd[:, u % 3], ps[:, at:at + 2, 0:AW], ACT.Abs).then_inc(s_abs, 1)
                act.wait_ge(nm_t, b + 1)
                nc.scalar.activation(nmT[:, :, :], ps[0:T, 0, 0:256].rearrange("p (r n) -> p r n", r=2), ACT.Copy)\
                    .then_inc(nm_copied, 1)
                with act.Fori(0, THIRDS) as third:
                    with act.Fori(0, T // 2) as i:
                        for k in range(4):
                            at = b * B_UNITS + third * (2 * T) + i * 4 + k
                            act.wait_ge(st_mm, at + 1)
                            act.wait_ge(p_used, at + (1 + B_CREDIT - 4))
                            act.wait_ge(p_summed, at + (1 + B_CREDIT - 4))
                            nc.scalar.activation(p0[:, k, :], unit(k).rearrange("p a n -> p (a n)"), ACT.Exp)\
                                .then_inc(p_exp, 1)
                    act.wait_ge(z_mm, b * THIRDS + third + 1)
                    nc.scalar.activation(z_sb[:, :, 0:QD], ps[:, 0:2, 0:QD], ACT.Copy).then_inc(z_copied, 1)
                    nc.scalar.activation(z_sb[:, :, QD:QW], ps[:, 6:8, QW:2 * QW - QD], ACT.Copy).then_inc(z_rest, 1)
                project_hi(b, jobs1, len(jobs0))

                def copy_fill(pair, parity, f, early):
                    e = evac_slot(parity, f)
                    n = ACT_FILLS.index(f)
                    act.wait_ge(fill_mm, b * (PAIRS * FILLS) + pair * FILLS + (f + 1))
                    if not (early and n < 2):
                        act.wait_ge(fill_pool, b * (PAIRS * len(ACT_FILLS)) + pair * len(ACT_FILLS) + (n - 1))
                    nc.scalar.activation(evac[:, e, :], ps[:, fill_bank(parity, f), :], ACT.Copy)\
                        .then_inc(fill_copied, 1)

                def step(pair, parity, main, tail):
                    for s in range(STEPS):
                        tile, j = ORDER[s]
                        act.wait_ge(t_max, b * (PAIRS * STEPS) + pair * STEPS + (s + 1))
                        shared = tile == 1 and j in SHARED
                        if main if shared else tail:
                            act.wait_ge(fill_mm, b * (PAIRS * FILLS) + pair * FILLS
                                        + (LAST_FILL[j] + 1 - (1 if shared else 2) * FILLS))
                        st = stat[:, tile, :]
                        nc.scalar.activation(p1[:, p1_slot(parity, tile, j), :],
                                             chunk_scores(s).rearrange("p a n -> p (a n)"),
                                             ACT.Exp, bias=st[:, NM + j:NM + j + 1],
                                             accum_out=st[:, SS + j:SS + j + 1]).then_inc(t_exp, 1)
                        if s % NJ == NJ - 1:
                            act.wait_ge(m_min, b * T + pair * 2 + (tile + 1))
                            nc.scalar.activation(st[:, EE:EE + NJ], st[:, NM:NM + NJ], ACT.Exp,
                                                 bias=st[:, MIN:MIN + 1], scale=-1.0).then_inc(m_exp, 1)
                        for back, hf in half_fills(s, main, tail):
                            if hf % 2 and hf // 2 in ACT_FILLS:
                                copy_fill(pair - back, (parity + back) % 2, hf // 2, back == 1 and not tail)

                pair_steps(act, step)
                for back, hf in FLUSH:
                    if hf % 2 and hf // 2 in ACT_FILLS:
                        copy_fill(PAIRS - back, (PAIRS - back) % 2, hf // 2, False)

        @block.vector
        def _(dve):
            def project_lo(b, jobs, base, hi_base):
                his = 0
                for k, (name, h, c) in enumerate(jobs):
                    if name in "gv":
                        bias, wide, dst = (W_BG, D, gT) if name == "g" else (W_BV, 64, vT)
                        n = TB * D // wide
                        at = (h * TH + c) * wide
                        dve.wait_ge(proj_mm, b * JOBS + (base + k + 1))
                        nc.vector.tensor_tensor(
                            dst[:, at:at + n * wide].rearrange("p (t d) -> p t d", d=wide),
                            ps[:, k % 8, 0:n * wide].rearrange("p (t d) -> p t d", d=wide),
                            w[:, bias:bias + wide].unsqueeze(1).broadcast_to((128, n, wide)),
                            ALU.add).then_inc(proj_lo, 1)
                        continue
                    his += 1
                    dst, lo, bias = split_target(name, h, c)
                    r = slice(D * lo, D * lo + D)
                    dve.wait_ge(proj_hi, b * HI_JOBS + (hi_base + his))
                    if bias is None:
                        ins = nc.vector.tensor_tensor(dst[r, :], ps[r, k % 8, :], dst[r, :].bitcast(F32), ALU.subtract)
                    else:
                        ins = nc.vector.scalar_tensor_tensor(
                            out=dst[r, :], in0=ps[r, k % 8, :], scalar=w[r, bias:bias + 1],
                            in1=dst[r, :].bitcast(F32), op0=ALU.add, op1=ALU.subtract)
                    ins.then_inc(proj_lo, 1)

            dve.sem_inc(p_summed, B_CREDIT)
            dve.wait_ge(w_in, 16)
            for h in range(2):
                r = slice(64 * h, 64 * h + 64)
                wp = w[r, W_P + h * P3:W_P + (h + 1) * P3]
                for k in range(2):
                    nc.vector.tensor_scalar(w_half[r, k, :], wp, -0.5 if h and k else 0.5, None, ALU.mult)\
                        .then_inc(w_half_done, 1)
            with dve.Fori(0, B) as b:
                project_lo(b, jobs0, 0, 0)
                with dve.Fori(0, T // 2) as i:
                    for u in range(2 * AU):
                        dve.wait_ge(s_mm, b * A_UNITS + i * (2 * AU) + (u + 1))
                        dve.wait_ge(s_abs, b * A_UNITS + i * (2 * AU) + (u + 1 + A_CREDIT))
                        apart(dve)
                        at = 4 * (u % 2)
                        nc.vector.tensor_tensor_reduce(
                            out=absd[:, u % 3], in0=ps[:, at:at + 2, 0:AW], in1=absd[:, u % 3], scale=1.0,
                            scalar=-3.0e38, op0=ALU.add, op1=ALU.max,
                            accum_out=part[:, u // AU, u % AU:u % AU + 1]).then_inc(s_max, 1)
                        if u % AU == AU - 1:
                            dve.wait_ge(s_max, b * A_UNITS + i * (2 * AU) + (u + 1 + A_CREDIT))
                            nc.vector.tensor_reduce(negmax[:, bass.ds(i * 2 + u // AU, 1)], part[:, u // AU, :],
                                                    AX.X, ALU.max, negate=True).then_inc(nm_tile, 1)
                dve.wait_ge(nm_tile, b * T + T)
                nc.vector.tensor_copy(nmh[:, :], negmax[:, :]).then_inc(nm_step, 1)
                dve.wait_ge(nm_step, b * 2 + 1)
                nc.vector.tensor_tensor(nml[:, :], negmax[:, :], nmh[:, :].bitcast(F32), ALU.subtract)\
                    .then_inc(nm_step, 1)
                with dve.Fori(0, THIRDS) as third:
                    nc.vector.memset(ps[:, 6:8, 0:2 * QW - QD], 0.0).then_inc(o_zero, 1)
                    dve.wait_ge(sums_zero, b * THIRDS + third + 1)
                    apart(dve)
                    with dve.Fori(0, T // 2) as i:
                        for k in range(4):
                            dve.wait_ge(p_exp, b * B_UNITS + third * (2 * T) + i * 4 + (k + 1))
                            dve.wait_ge(p_summed, b * B_UNITS + third * (2 * T) + i * 4 + (k - 1 + B_CREDIT))
                            sums = psum_p[:, k % 2]
                            mine = p0[:, k, :].rearrange("p (g q) -> p g q", g=4)[:, :, 0:QD]
                            nc.vector.tensor_tensor(sums, mine, sums, ALU.add).then_inc(p_summed, 1)
                    dve.wait_ge(z_copied, b * THIRDS + third + 1)
                    dve.wait_ge(z_rest, b * THIRDS + third + 1)
                    nc.vector.reciprocal(z_sb[:, :, :], z_sb[:, :, :]).then_inc(z_inv, 1)
                    dve.wait_ge(z_inv, b * THIRDS + third + 1)
                    nc.vector.tensor_tensor(yn[:, bass.ds(third * 2, 2), :], ps[:, 6:8, 0:QW], z_sb[:, :, :],
                                            ALU.mult).then_inc(y_done, 1)
                    dve.wait_ge(y_done, b * THIRDS + third + 1)
                    apart(dve)
                for k in range(H // QW):
                    dve.wait_ge(wo_mm, b * (H // QW) + (k + 1))
                    xs = x_sb[:, k * QW:(k + 1) * QW]
                    nc.vector.scalar_tensor_tensor(out=xs, in0=ps[:, k % 8, 0:QW], scalar=w[:, W_BO:W_BO + 1],
                                                   in1=xs, op0=ALU.add, op1=ALU.add).then_inc(x1_done, 1)
                project_lo(b, jobs1, len(jobs0), HI_JOBS0)

                FIRST = BY_DVE[0]

                def add_fill(pair, parity, f, first):
                    dve.wait_ge(fill_mm, b * (PAIRS * FILLS) + pair * FILLS + (f + 1))
                    n = BY_DVE.index(f)
                    if not first:
                        dve.wait_ge(fill_dve, b * (PAIRS * len(BY_DVE)) + pair * len(BY_DVE) + n)
                    xs = x_sb[:, f * BANK:(f + 1) * BANK]
                    nc.vector.tensor_tensor(xs, ps[:, fill_bank(parity, f), :], xs, ALU.add).then_inc(fill_dve, 1)

                def factors(pair, tile, early):
                    st = stat[:, tile, :]
                    dve.wait_ge(m_exp, b * T + pair * 2 + (tile + 1))
                    nc.vector.tensor_tensor_reduce(out=st[:, ES:ES + NJ], in0=st[:, EE:EE + NJ], in1=st[:, SS:SS + NJ],
                                                   scale=1.0, scalar=0.0, op0=ALU.mult, op1=ALU.add,
                                                   accum_out=st[:, SUM:SUM + 1]).then_inc(m_sum, 1)
                    dve.wait_ge(m_sum, b * T + pair * 2 + (tile + 1))
                    nc.vector.reciprocal(st[:, INV:INV + 1], st[:, SUM:SUM + 1]).then_inc(m_inv, 1)
                    dve.wait_ge(m_inv, b * T + pair * 2 + (tile + 1))
                    if not early:
                        dve.wait_ge(vw_done, b * T + pair * 2 + (tile - 1))
                    nc.vector.tensor_scalar(st[:, WW:WW + NJ], st[:, EE:EE + NJ], st[:, INV:INV + 1], None, ALU.mult)\
                        .then_inc(m_fac, 1)

                def step(pair, parity, main, tail):
                    for s in range(STEPS):
                        tile, j = ORDER[s]
                        st = stat[:, tile, :]
                        dve.wait_ge(t_mm, b * (PAIRS * STEPS) + pair * STEPS + (s + 1))
                        nc.vector.tensor_reduce(st[:, NM + j:NM + j + 1], chunk_scores(s)
                                                .rearrange("p a n -> p (a n)"), AX.X, ALU.max, negate=True)\
                            .then_inc(t_max, 1)
                        if s % NJ == NJ - 1:
                            dve.wait_ge(t_max, b * (PAIRS * STEPS) + pair * STEPS + (s + 1))
                            nc.vector.tensor_reduce(st[:, MIN:MIN + 1], st[:, NM:NM + NJ], AX.X, ALU.min)\
                                .then_inc(m_min, 1)
                        if s == 0 and main:
                            factors(pair - 1, 1, not tail)
                        if s == NJ:
                            factors(pair, 0, not main)
                        for back, hf in half_fills(s, main, tail):
                            if hf % 2 and hf // 2 in BY_DVE:
                                add_fill(pair - back, (parity + back) % 2, hf // 2, not tail and hf // 2 == FIRST)

                pair_steps(dve, step)
                factors(PAIRS - 1, 1, False)
                for back, hf in FLUSH:
                    if hf % 2 and hf // 2 in BY_DVE:
                        add_fill(PAIRS - back, (PAIRS - back) % 2, hf // 2, False)

        @block.gpsimd
        def _(pool):
            nc.gpsimd.memset(ident[:, :], 0.0).then_inc(id_zero, 1)
            pool.wait_ge(id_zero, 1)
            nc.gpsimd.affine_select(out=ident[:, :], in_=ident[:, :], compare_op=ALU.not_equal, fill=1.0, base=0,
                                    pattern=[[-1, 128]], channel_multiplier=1).then_inc(const_done, 1)
            nc.gpsimd.memset(ones[:, :], 1.0).then_inc(const_done, 1)
            pool.wait_ge(const_done, 2)
            nc.gpsimd.memset(kslot[P3:K].bitcast(F32), 0.0).then_inc(const_done, 1)
            pool.wait_ge(const_done, 3)
            with pool.Fori(0, B) as b:
                for n, rest in enumerate((psd, thslot, th, ph)):
                    nc.gpsimd.memset(rest[P3:K].bitcast(F32), 0.0).then_inc(rest_zero, 1)
                pool.wait_ge(rest_zero, b * 4 + 4)
                apart(pool)
                nc.gpsimd.memset(ph[P3:P3 + 2, :].bitcast(F32), 1.0).then_inc(ones_set, 1)
                pool.wait_ge(ones_set, b + 1)
                pool.wait_ge(nm_in, b * 32 + 32)
                apart(pool)
                with pool.Fori(0, THIRDS) as third:
                    nc.gpsimd.memset(psum_p[:, :, :, :], 0.0).then_inc(sums_zero, 1)
                    pool.wait_ge(z_mm, b * THIRDS + third + 1)
                    apart(pool)
                pool.wait_ge(x1_done, b * (H // QW) + H // QW)
                apart(pool)
                nc.gpsimd.memset(qst[P3:K].bitcast(F32), 0.0).then_inc(q_zero, 1)
                pool.wait_ge(q_zero, b + 1)

                FIRST = ACT_FILLS[0]

                def add_fill(pair, parity, f, first):
                    n = ACT_FILLS.index(f)
                    count = b * (PAIRS * len(ACT_FILLS)) + pair * len(ACT_FILLS) + (n + 1)
                    pool.wait_ge(fill_copied, count)
                    if not first:
                        pool.wait_ge(fill_pool, count - 1)
                    xs = x_sb[:, f * BANK:(f + 1) * BANK]
                    nc.gpsimd.tensor_tensor(xs, evac[:, evac_slot(parity, f), :], xs, ALU.add).then_inc(fill_pool, 1)

                def weigh_v(pair, parity, tile):
                    pool.wait_ge(m_fac, b * T + pair * 2 + (tile + 1))
                    pool.wait_ge(v_in[parity], b * (8 * PAIRS) + (pair - parity) * 8 + 16)
                    nc.gpsimd.tensor_tensor(
                        vw[:, 2 * parity + tile],
                        vslot[:, parity, 64 * tile:64 * tile + 64].unsqueeze(1).broadcast_to((128, NJ, 64)),
                        stat[:, tile, WW:WW + NJ].unsqueeze(2).broadcast_to((128, NJ, 64)),
                        ALU.mult).then_inc(vw_done, 1)

                def step(pair, parity, main, tail):
                    for s in range(STEPS):
                        if s == 0 and main:
                            weigh_v(pair - 1, 1 - parity, 1)
                        if s == NJ:
                            weigh_v(pair, parity, 0)
                        for back, hf in half_fills(s, main, tail):
                            if hf % 2 and hf // 2 in ACT_FILLS:
                                add_fill(pair - back, (parity + back) % 2, hf // 2, not tail and hf // 2 == FIRST)

                pair_steps(pool, step)
                weigh_v(PAIRS - 1, (PAIRS - 1) % 2, 1)
                for back, hf in FLUSH:
                    if hf % 2 and hf // 2 in ACT_FILLS:
                        add_fill(PAIRS - back, (PAIRS - back) % 2, hf // 2, False)
                pool.wait_ge(fill_pool, b * (PAIRS * len(ACT_FILLS)) + PAIRS * len(ACT_FILLS))
                apart(pool)


def pack_weights(Wg, bg, Wt, bt, Wp, bp, Wo, bo, Wq, bq, Wk, bk, Wv, bv):
    import numpy as np

    pack = np.zeros((128, W_COLS), np.float32)

    def stack(col, bias_col, W, b):
        for block in range(3):
            for half in range(2):
                at = col + half * P3 + D * block
                pack[64 * half:64 * half + 64, at:at + W.shape[0]] = W.T
            pack[D * block:D * block + W.shape[0], bias_col] = b

    stack(W_T, W_BT, Wt, bt)
    stack(W_P, W_BP, Wp, bp)
    stack(W_Q, W_BQ, Wq, bq)
    stack(W_K, W_BK, Wk, bk)
    for half in range(2):
        rows = slice(64 * half, 64 * half + 64)
        pack[rows, W_G:W_G + D] = Wg.T
        pack[rows, W_V:W_V + 64] = Wv.T
        pack[rows, W_BO] = bo
    for group in range(4):
        pack[D * group:D * group + D, W_O + 64 * group:W_O + 64 * group + 64] = Wo.T
    pack[:, W_BG:W_BG + D] = bg
    pack[:, W_BV:W_BV + 64] = bv
    return pack


def kernel(**inputs):
    import numpy as np
    import concourse.bacc as bacc
    from concourse.bass_utils import run_bass_kernel_spmd

    a = {k: np.asarray(v) for k, v in inputs.items()}
    B, C, HH, WWD = a["x"].shape
    arrays = {
        "x": np.ascontiguousarray(a["x"]).reshape(B, C, HH * WWD),
        "wpack": pack_weights(*[a[f"L0_conv_{n}"] for n in ("Wg", "bg", "Wt", "bt", "Wp", "bp", "Wo", "bo")],
                              *[a[f"L1_conv_{n}"] for n in ("Wq", "bq", "Wk", "bk", "Wv", "bv")]),
    }
    nc = bacc.Bacc("TRN2", target_bir_lowering=False, num_devices=1)
    aps = [nc.dram_tensor(n, v.shape, mybir.dt.from_np(v.dtype), kind="ExternalInput").ap() for n, v in arrays.items()]
    out = nc.dram_tensor("out", (B, C, HH * WWD), F32, kind="ExternalOutput").ap()
    attention_kernel(nc, *aps, out)
    r = run_bass_kernel_spmd(nc, [arrays], core_ids=[0])
    return r.results[0]["out"].reshape(B, C, HH, WWD)
```

```python
from contextlib import ExitStack

import concourse.bass as bass
from concourse import mybir

F32 = mybir.dt.float32
F32R = mybir.dt.float32r
ALU = mybir.AluOpType
ACT = mybir.ActivationFunctionType
AX = mybir.AxisListType

BANK = 512
D = 32
DQ = 8
P3 = 3 * D
K = 128

W_T, W_P = 0, 2 * P3
W_Q, W_K = 4 * P3, 5 * P3
W_G = 6 * P3
W_V = W_G + 2 * D
W_O = W_V + 2 * 64
W_BG = W_O + 4 * 64
W_BV = W_BG + D
W_BT = W_BV + 64
W_BP, W_BQ, W_BK, W_BO = W_BT + 1, W_BT + 2, W_BT + 3, W_BT + 4
W_COLS = W_BT + 5


def attention_kernel(nc, x, wpack, out):
    B, C, N = x.shape
    H = N // 2
    T = N // 128
    TH = T // 2
    CH = H // BANK
    assert C == 64 and H % BANK == 0 and N % 128 == 0

    PARTS = 3
    PW = H // PARTS

    AU = -(-H // (2 * BANK))
    AW = [H // (4 * AU) * 2 + 2 * (u < H % (4 * AU) // 4) for u in range(AU)]
    A_AT = [2 * sum(AW[:u]) for u in range(AU)]
    assert 2 * sum(AW) == H and max(AW) <= BANK
    A_SLOTS = 4
    UW = 3 * BANK
    THIRDS = 3
    THW = N // THIRDS
    assert THW == 2 * UW
    QW = UW // 4
    QD = 352
    B_SLOTS = 4
    PAIRS = T // 2
    JW = 2 * BANK
    NJ = N // JW
    FILLS = CH
    STEPS = 2 * NJ
    assert STEPS == 2 * FILLS and STEPS % 3 == 0
    LAG = 3

    def chunk_of(c, f):
        return (c * CH + f) // 2, (c * CH + f) % 2

    LAST_FILL = [max(f for c in range(2) for f in range(FILLS) if chunk_of(c, f)[0] == j) for j in range(NJ)]
    BY_USE = sorted(range(NJ), key=lambda j: LAST_FILL[j])
    SHARED = BY_USE[:4]
    ORDER = [(0, j) for j in BY_USE] + [(1, j) for j in BY_USE[4:] + SHARED]
    assert all(2 * LAST_FILL[j] + 1 + LAG < STEPS - len(SHARED) for j in SHARED)
    BY_DVE = (1, 5)

    ctx = ExitStack()
    with ctx:
        def sb(name, shape, dt=F32, stack=ctx):
            return stack.enter_context(nc.sbuf_tensor(name, shape, dt))

        def sem(name):
            return ctx.enter_context(nc.semaphore(name))

        w = sb("w", [128, W_COLS])
        w_half = sb("w_half", [128, 2, P3])
        ident = sb("ident", [128, 128])
        ones = sb("ones", [128, D])
        x_sb = sb("x_sb", [128, H])
        stat = sb("stat", [128, 2, 54])
        evac = sb("evac", [128, 2, BANK])
        kslot = sb("kslot", [K, 2, 2, 256], F32R)
        vslot = sb("vslot", [128, 2, 128])
        vw = sb("vw", [128, 4, NJ, 64])

        with ExitStack() as l0:
            th = sb("th", [K, N], F32R, l0)
            ph = sb("ph", [K, N], F32R, l0)
            gT = sb("gT", [128, T * D], F32, l0)
            phslot = sb("phslot", [K, B_SLOTS, 128], F32R, l0)
            gslot = sb("gslot", [128, B_SLOTS, D], F32, l0)
            negmax = sb("negmax", [128, 1 + T], F32, l0)
            nmh = sb("nmh", [128, T], F32R, l0)
            nml = sb("nml", [128, T], F32, l0)
            nmT = sb("nmT", [T, 2, 128], F32R, l0)
            with ExitStack() as pass_a:
                psd = sb("psd", [K, 2, H], F32R, pass_a)
                thslot = sb("thslot", [K, A_SLOTS, 128], F32R, pass_a)
                absd = sb("absd", [128, AU, 2, BANK], F32, pass_a)
                part = sb("part", [128, 4, AU], F32, pass_a)
            with ExitStack() as pass_b:
                p0 = sb("p0", [128, 4, UW], F32, pass_b)
                psum_p = sb("psum_p", [128, 2, 4, QD], F32, pass_b)
                z_sb = sb("z_sb", [128, 2, QW], F32, pass_b)
                yn = sb("yn", [128, 2 * THIRDS, QW], F32, pass_b)
        with ExitStack() as l1:
            qst = sb("qst", [K, H], F32R, l1)
            kst = sb("kst", [P3, H], F32R, l1)
            p1 = sb("p1", [128, 3 * NJ, JW], F32, l1)
            with ExitStack() as build:
                vT = sb("vT", [128, T * 64], F32, build)
            p1_late = sb("p1_late", [128, NJ - len(SHARED), JW], F32, l1)

        def p1_slot(parity, tile, j):
            if tile == 0:
                return p1[:, parity * NJ + j, :]
            if j in SHARED:
                return p1[:, 2 * NJ + SHARED.index(j), :]
            late = BY_USE[len(SHARED):].index(j)
            return p1_late[:, late, :] if parity else p1[:, 2 * NJ + len(SHARED) + late, :]

        vT_d = nc.dram_tensor("vT_d", [128, T * 64], F32, kind="Internal").ap()

        ps = ctx.enter_context(nc.psum_tensor("ps", [128, 8, BANK], F32))

        w_in, x_in = sem("w_in"), [sem(f"x_in{k}") for k in range(PARTS)]
        waited = sem("waited")
        id_zero, const_done = sem("id_zero"), sem("const_done")
        w_half_done = sem("w_half_done")
        proj_mm, proj_hi, proj_lo = sem("proj_mm"), sem("proj_hi"), sem("proj_lo")
        th_in = [sem(f"th_in{s}") for s in range(A_SLOTS)]
        d_mm, s_mm, s_abs, s_max = sem("d_mm"), sem("s_mm"), sem("s_abs"), sem("s_max")
        nm_tile, nm_step, nm_t, nm_copied, nm_in = sem("nm_tile"), sem("nm_step"), sem("nm_t"), sem("nm_copied"), sem("nm_in")
        slot_in = [sem(f"slot_in{s}") for s in range(B_SLOTS)]
        st_mm, p_exp, p_summed, p_used = sem("st_mm"), sem("p_exp"), sem("p_summed"), sem("p_used")
        rest_zero, ones_set, q_zero, o_zero, y_copied, z_mm, z_copied, z_inv, y_done = sem("rest_zero"), sem("ones_set"), sem("q_zero"), sem("o_zero"), sem("y_copied"), sem("z_mm"), sem("z_copied"), sem("z_inv"), sem("y_done")
        wo_mm, x1_done = sem("wo_mm"), sem("x1_done")
        vT_out = sem("vT_out")
        k_in = [sem(f"k_in{s}") for s in range(2)]
        v_in = [sem(f"v_in{s}") for s in range(2)]
        t_mm, t_max, t_exp = sem("t_mm"), sem("t_max"), sem("t_exp")
        m_min, m_exp, m_sum, m_inv, m_fac, vw_done = sem("m_min"), sem("m_exp"), sem("m_sum"), sem("m_inv"), sem("m_fac"), sem("vw_done")
        fill_mm, fill_copied, fill_dve, fill_pool = sem("fill_mm"), sem("fill_copied"), sem("fill_dve"), sem("fill_pool")
        result_out = [sem(f"result_out{k}") for k in range(PARTS)]

        GT, VT = 6, 4
        jobs0 = ([("theta", h, c) for c in range(CH) for h in range(2)]
                 + [("sum", 0, c) for c in range(CH)] + [("diff", 0, c) for c in range(CH)]
                 + [("phi", h, c) for h in range(2) for c in range(CH)]
                 + [("g", 0, t) for t in range(0, TH, GT)])
        jobs1 = ([("k", 0, c) for c in range(CH)]
                 + [("v", 0, t) for t in range(0, TH, VT)]
                 + [("q", 0, c) for c in range(CH)])
        K_JOBS = len(jobs0) + CH
        V_JOBS = K_JOBS + TH // VT
        JOBS = len(jobs0) + len(jobs1)
        HI_JOBS = sum(n not in "gv" for n, _, _ in jobs0 + jobs1)
        HI_JOBS0 = sum(n not in "gv" for n, _, _ in jobs0)
        stacks = {
            "theta": (th, W_T, 1, W_BT), "phi": (ph, W_P, 2, W_BP),
            "q": (qst, W_Q, 1, W_BQ), "k": (kst, W_K, 2, W_BK),
        }

        def split_target(name, h, c):
            if name in ("sum", "diff"):
                return psd[0:P3, int(name == "diff"), c * BANK:(c + 1) * BANK], 2, W_BP if name == "sum" else None
            dst, _, lo, bias = stacks[name]
            return dst[0:P3, h * H + c * BANK:h * H + (c + 1) * BANK], lo, bias

        NM_TILE = 1 + 2 * (T // 4) + 1
        K_LOADS = 6

        A_CREDIT = AU
        B_CREDIT = 2 * B_SLOTS
        A_UNITS, B_UNITS = T * AU, THIRDS * T * 2

        def unit(k):
            return ps[:, 3 * (k % 2):3 * (k % 2) + 3, :]

        def half_fills(s, main, tail):
            if s < LAG:
                return [(2, STEPS - LAG + s)] if tail else []
            return [(1, s - LAG)] if main else []

        FLUSH = [(2, k) for k in range(STEPS - LAG, STEPS)] + [(1, k) for k in range(STEPS)]
        ACT_FILLS = [f for f in range(FILLS) if f not in BY_DVE]

        def chunk_scores(s):
            return ps[:, 2 * (s % 3):2 * (s % 3) + 2, :]

        def fill_bank(parity, f):
            return 6 + (parity + f) % 2

        def evac_slot(parity, f):
            return (parity * len(ACT_FILLS) + ACT_FILLS.index(f)) % 2

        NM, SS, EE, WW, ES, MIN, SUM, INV = 0, 10, 20, 30, 40, 50, 51, 52

        def pair_steps(eng, step):
            step(0, 0, False, False)
            step(1, 1, True, False)
            with eng.Fori(0, PAIRS // 2 - 1) as i:
                for parity in range(2):
                    step(i * 2 + (2 + parity), parity, True, True)

        def apart(eng):
            eng.sem_inc(waited, 1)

        block = ctx.enter_context(nc.Block())

        @block.sync
        def _(sp):
            def copy_words(to, of):
                return sp.dma_start(to.bitcast(F32), of.bitcast(F32))

            sp.dma_start(w[:, :], wpack).then_inc(w_in, 16)
            sp.sem_inc(p_used, B_CREDIT)
            def load_x(b, k):
                for h in range(2):
                    sp.dma_start(x_sb[64 * h:64 * h + 64, k * PW:(k + 1) * PW],
                                 x[bass.ds(b, 1), :, h * H + k * PW:h * H + (k + 1) * PW]
                                 .rearrange("a c n -> (a c) n")).then_inc(x_in[k], 16)

            def store_result(b, k):
                done = (k + 1) * FILLS // PARTS
                for by, mine in ((fill_dve, BY_DVE), (fill_pool, ACT_FILLS)):
                    sp.wait_ge(by, b * (PAIRS * len(mine)) + (PAIRS - 1) * len(mine) + sum(f < done for f in mine))
                    apart(sp)
                for h in range(2):
                    sp.dma_start(out[bass.ds(b, 1), :, h * H + k * PW:h * H + (k + 1) * PW]
                                 .rearrange("a c n -> (a c) n"),
                                 x_sb[64 * h:64 * h + 64, k * PW:(k + 1) * PW]).then_inc(result_out[k], 16)

            def layers(b):
                def load_theta(s, tile):
                    copy_words(thslot[0:P3, s, :], th[0:P3, bass.ds(tile * 128, 128)]).then_inc(th_in[s], 16)

                sp.wait_ge(proj_lo, b * JOBS + 2 * CH)
                for s in range(A_SLOTS):
                    load_theta(s, s)
                with sp.Fori(0, T // A_SLOTS - 1) as i:
                    for s in range(A_SLOTS):
                        sp.wait_ge(s_mm, b * A_UNITS + i * (A_SLOTS * AU) + (s + 1) * AU)
                        load_theta(s, i * A_SLOTS + (A_SLOTS + s))
                def load_slots(third, i):
                    for s in range(B_SLOTS):
                        sp.wait_ge(p_used, b * B_UNITS + third * (2 * T) + i * (2 * B_SLOTS) + 2 * (s + 1))
                        copy_words(phslot[:, s, :], ph[:, bass.ds(i * (B_SLOTS * 128) + s * 128, 128)])\
                            .then_inc(slot_in[s], 16)
                        sp.dma_start(gslot[:, s, :], gT[:, bass.ds(i * (B_SLOTS * D) + s * D, D)])\
                            .then_inc(slot_in[s], 16)

                def load_other_slots(third):
                    with sp.Fori(0, T // B_SLOTS - 1) as i:
                        load_slots(third, i + 1)

                sp.wait_ge(ones_set, b + 1)
                load_slots(0, 0)
                sp.wait_ge(nm_copied, b + 1)
                for r in range(2):
                    copy_words(th[P3 + r:P3 + r + 1, :].rearrange("a (t n) -> a t n", n=128), nmT[:, r, :]).then_inc(nm_in, 16)
                with sp.Fori(0, THIRDS - 1) as third:
                    load_other_slots(third)
                    load_slots(third + 1, 0)
                load_other_slots(THIRDS - 1)
                def load_k(s, half, cols):
                    for v in range(2):
                        for block in range(3):
                            to, at = D * block + DQ * v, D * block + DQ * half
                            sp.dma_start(kslot[to:to + DQ, s, v, :].bitcast(F32),
                                         kst[at:at + DQ, cols].bitcast(F32))\
                                .then_inc(k_in[s], 16)

                sp.wait_ge(proj_lo, b * JOBS + K_JOBS)
                for s in range(2):
                    load_k(s, 0, slice(s * 256, (s + 1) * 256))
                sp.wait_ge(proj_lo, b * JOBS + V_JOBS)
                for s in range(2):
                    sp.dma_start(vslot[:, s, :], vT[:, s * 128:(s + 1) * 128]).then_inc(v_in[s], 16)
                sp.dma_start(vT_d, vT[:, :]).then_inc(vT_out, 16)
                sp.wait_ge(vT_out, b * 16 + 16)
                apart(sp)
                for half, first in ((0, 2), (1, 0)):
                    with sp.Fori(0, (PAIRS // 2 - first) // 2) as i:
                        for s in range(2):
                            pair = half * (PAIRS // 2) + first + s
                            sp.wait_ge(vw_done, b * T + i * 4 + 2 * (pair - 1))
                            load_k(s, half, bass.ds(i * 512 + (first + s) * 256, 256))
                            sp.dma_start(vslot[:, s, :], vT_d[:, bass.ds(i * 256 + pair * 128, 128)])\
                                .then_inc(v_in[s], 16)

            for k in range(PARTS):
                load_x(0, k)
            with sp.Fori(0, B - 1) as b:
                layers(b)
                for k in range(PARTS + 1):
                    if k < PARTS:
                        store_result(b, k)
                    if k > 0:
                        sp.wait_ge(result_out[k - 1], b * 32 + 32)
                        apart(sp)
                        load_x(b + 1, k - 1)
            layers(B - 1)
            for k in range(PARTS):
                store_result(B - 1, k)
            for k in range(PARTS):
                sp.wait_ge(result_out[k], B * 32)

        @block.tensor
        def _(pe):
            def project(b, jobs, base):
                for k, (name, h, c) in enumerate(jobs):
                    if k >= 8:
                        pe.wait_ge(proj_lo, b * JOBS + (base + k - 7))
                    if base == 0 and k % (2 * CH // PARTS) == 0 and k < 2 * CH:
                        pe.wait_ge(x_in[k // (2 * CH // PARTS)], b * 32 + 32)
                    o = ps[:, k % 8, :]
                    if name in ("sum", "diff"):
                        mm = nc.tensor.matmul(o[0:P3, :], w_half[:, int(name == "diff"), :],
                                              x_sb[:, c * BANK:(c + 1) * BANK], start=True, stop=True)
                    elif name in stacks:
                        col = stacks[name][1]
                        mm = nc.tensor.matmul(o[0:P3, :], w[:, col + h * P3:col + (h + 1) * P3],
                                              x_sb[:, c * BANK:(c + 1) * BANK], start=True, stop=True)
                    else:
                        col, wide, tiles = (W_G, 2 * D, GT) if name == "g" else (W_V, 2 * 64, VT)
                        for t in range(tiles):
                            mm = nc.tensor.matmul(o[:, t * wide:(t + 1) * wide],
                                                  x_sb[:, (c + t) * 128:(c + t + 1) * 128],
                                                  w[:, col:col + wide], start=True, stop=True)
                    mm.then_inc(proj_mm, 1)

            pe.sem_inc(s_max, A_CREDIT)
            pe.sem_inc(s_abs, A_CREDIT)
            pe.sem_inc(z_mm, 1)
            pe.wait_ge(w_half_done, 4)
            pe.wait_ge(const_done, 3)
            with pe.Fori(0, B) as b:
                project(b, jobs0, 0)
                pe.wait_ge(proj_lo, b * JOBS + len(jobs0))
                pe.wait_ge(rest_zero, b * 4 + 4)
                apart(pe)

                def half_unit(k, s, u):
                    for c in range(2):
                        col = A_AT[u] + c * AW[u]
                        mm = nc.tensor.matmul(ps[:, 4 * ((s * AU + u) % 2) + 2 * k + c, 0:AW[u]],
                                              thslot[:, s, :], psd[:, k, col:col + AW[u]], start=True, stop=True)
                    mm.then_inc(d_mm if k else s_mm, 1)

                def first_differences(i, s):
                    pe.wait_ge(th_in[s], b * (16 * T // A_SLOTS) + i * 16 + 16)
                    pe.wait_ge(s_abs, b * A_UNITS + i * (A_SLOTS * AU) + (s * AU + A_CREDIT - 1))
                    half_unit(1, s, 0)

                def score_tiles(i, last):
                    for s in range(A_SLOTS):
                        at = b * A_UNITS + i * (A_SLOTS * AU) + s * AU
                        for u in range(AU):
                            if u + 1 < AU:
                                pe.wait_ge(s_abs, at + (u + 1 + A_CREDIT - 1))
                                half_unit(1, s, u + 1)
                            elif s + 1 < A_SLOTS:
                                first_differences(i, s + 1)
                            elif not last:
                                first_differences(i + 1, 0)
                            pe.wait_ge(s_max, at + (u + A_CREDIT - 1))
                            half_unit(0, s, u)

                first_differences(0, 0)
                apart(pe)
                with pe.Fori(0, T // A_SLOTS - 1) as i:
                    score_tiles(i, False)
                score_tiles(T // A_SLOTS - 1, True)
                pe.wait_ge(nm_step, b * 2 + 2)
                nc.tensor.transpose(ps[0:T, 0, 0:128], nmh[:, :].bitcast(F32), ident[:, :])
                nc.tensor.transpose(ps[0:T, 0, 128:256], nml[:, :], ident[:, :]).then_inc(nm_t, 1)
                pe.wait_ge(nm_copied, b + 1)
                pe.wait_ge(nm_in, b * 32 + 32)
                pe.wait_ge(ones_set, b + 1)
                apart(pe)
                with pe.Fori(0, THIRDS) as third:
                    def scores(i, k):
                        if k % 2 == 0:
                            pe.wait_ge(slot_in[k // 2 % B_SLOTS],
                                       b * (32 * THIRDS * T // B_SLOTS) + third * (32 * T // B_SLOTS) + i * 32
                                       + 32 * (k // (2 * B_SLOTS) + 1))
                        for c in range(3):
                            mm = nc.tensor.matmul(unit(k)[:, c, :], phslot[:, k // 2 % B_SLOTS, :],
                                                  th[:, bass.ds(third * THW + (k % 2 * UW + c * BANK), BANK)],
                                                  start=True, stop=True)
                        mm.then_inc(st_mm, 1)

                    def products(k):
                        for g in range(4):
                            nc.tensor.matmul(ps[D * g:D * g + D, 6 + k % 2, 0:QW],
                                             gslot[:, k // 2, :], p0[:, k % 4, g * QW:(g + 1) * QW],
                                             start=False, stop=False, skip_group_check=True)
                        for g in range(4):
                            mm = nc.tensor.matmul(ps[D * g:D * g + D, 6 + k % 2, QW:2 * QW - QD],
                                                  ones[:, :], p0[:, k % 4, g * QW + QD:(g + 1) * QW],
                                                  start=False, stop=False, skip_group_check=True)
                        mm.then_inc(p_used, 1)

                    def tiles(i, last):
                        for k in range(2 * B_SLOTS):
                            pe.wait_ge(p_exp, b * B_UNITS + third * (2 * T) + i * (2 * B_SLOTS) + (k + 1))
                            if not last or k + 2 < 2 * B_SLOTS:
                                scores(i, k + 2)
                            products(k)

                    scores(0, 0)
                    scores(0, 1)
                    pe.wait_ge(o_zero, b * (THIRDS + 1) + third + 1)
                    apart(pe)
                    with pe.Fori(0, T // B_SLOTS - 1) as i:
                        tiles(i, False)
                    tiles(T // B_SLOTS - 1, True)
                    pe.wait_ge(p_summed, b * B_UNITS + third * (2 * T) + (2 * T + B_CREDIT))
                    pe.wait_ge(y_copied, b * (2 * THIRDS) + third * 2 + 2)
                    for u in range(2):
                        for g in range(4):
                            mm = nc.tensor.matmul(ps[D * g:D * g + D, 6 + u, 0:QD], ones[:, :],
                                                  psum_p[:, u, g, :], start=True, stop=True)
                    mm.then_inc(z_mm, 1)
                pe.wait_ge(z_copied, b * THIRDS + THIRDS)
                pe.wait_ge(o_zero, b * (THIRDS + 1) + THIRDS + 1)
                for k in range(H // QW):
                    if k < 8 and k % 4 == 0:
                        pe.wait_ge(y_done, b * THIRDS + (THIRDS + k // 4))
                    if k >= 8:
                        pe.wait_ge(x1_done, b * (H // QW) + (k - 7))
                    for h in range(2):
                        mm = nc.tensor.matmul(ps[64 * h:64 * h + 64, k % 8, 0:QW],
                                              w[:, W_O + 64 * (k % 4):W_O + 64 * (k % 4 + 1)],
                                              yn[:, THIRDS * h + k // 4, :], start=True, stop=True)
                    mm.then_inc(wo_mm, 1)
                pe.wait_ge(x1_done, b * (H // QW) + H // QW)
                project(b, jobs1, len(jobs0))
                pe.wait_ge(proj_lo, b * JOBS + JOBS)
                pe.wait_ge(q_zero, b + 1)

                def half_fill(pair, parity, hf, early):
                    f, tile = hf // 2, hf % 2
                    bank = fill_bank(parity, f)
                    if hf < 2:
                        pe.wait_ge(vw_done, b * T + pair * 2 + (tile + 1))
                    if tile == 0 and not (early and f < 2):
                        back, g = (0, f - 2) if f >= 2 else (1, f + FILLS - 2)
                        mine, by = (BY_DVE, fill_dve) if g in BY_DVE else (ACT_FILLS, fill_copied)
                        pe.wait_ge(by, b * (PAIRS * len(mine)) + pair * len(mine)
                                   + (mine.index(g) + 1 - back * len(mine)))
                    for c in range(2):
                        j, part = chunk_of(c, f)
                        mm = nc.tensor.matmul(ps[64 * c:64 * c + 64, bank, :], vw[:, 2 * parity + tile, j, :],
                                              p1_slot(parity, tile, j)[:, part * BANK:(part + 1) * BANK],
                                              start=(tile == 0), stop=(tile == 1))
                    if tile == 1:
                        mm.then_inc(fill_mm, 1)

                def step(pair, parity, main, tail):
                    for s in range(STEPS):
                        if s == 0:
                            pe.wait_ge(k_in[parity], b * (K_LOADS * 8 * PAIRS) + (pair - parity) * (K_LOADS * 8) + K_LOADS * 16)
                        if s >= 3 or main:
                            pe.wait_ge(t_exp, b * (PAIRS * STEPS) + pair * STEPS + (s - 2))
                        tile, j = ORDER[s]
                        for c in range(2):
                            half, at = divmod(j * JW + c * BANK, H)
                            mm = nc.tensor.matmul(chunk_scores(s)[:, c, :],
                                                  kslot[:, parity, half, tile * 128:(tile + 1) * 128],
                                                  qst[:, at:at + BANK], start=True, stop=True)
                        mm.then_inc(t_mm, 1)
                        for back, hf in half_fills(s, main, tail):
                            half_fill(pair - back, (parity + back) % 2, hf, back == 1 and not tail)

                pair_steps(pe, step)
                for back, hf in FLUSH:
                    half_fill(PAIRS - back, (PAIRS - back) % 2, hf, False)
                pe.wait_ge(fill_copied, b * (PAIRS * len(ACT_FILLS)) + PAIRS * len(ACT_FILLS))
                pe.wait_ge(fill_dve, b * (PAIRS * len(BY_DVE)) + PAIRS * len(BY_DVE))

        @block.scalar
        def _(act):
            def project_hi(b, jobs, base):
                for k, (name, h, c) in enumerate(jobs):
                    if name in "gv":
                        continue
                    dst, _, bias = split_target(name, h, c)
                    act.wait_ge(proj_mm, b * JOBS + (base + k + 1))
                    if bias is None:
                        ins = nc.scalar.activation(dst, ps[0:P3, k % 8, :], ACT.Copy)
                    else:
                        ins = nc.scalar.activation(dst, ps[0:P3, k % 8, :], ACT.Identity,
                                                   bias=w[0:P3, bias:bias + 1])
                    ins.then_inc(proj_hi, 1)

            act.wait_ge(w_in, 16)
            with act.Fori(0, B) as b:
                project_hi(b, jobs0, 0)
                with act.Fori(0, T // 2) as i:
                    for u in range(2 * AU):
                        act.wait_ge(d_mm, b * A_UNITS + i * (2 * AU) + (u + 1))
                        act.wait_ge(s_max, b * A_UNITS + i * (2 * AU) + (u + 1 - AU + A_CREDIT))
                        at = 4 * (u % 2) + 2
                        n = AW[u % AU]
                        nc.scalar.activation(absd[:, u % AU, :, 0:n], ps[:, at:at + 2, 0:n], ACT.Abs).then_inc(s_abs, 1)
                act.wait_ge(nm_t, b + 1)
                nc.scalar.activation(nmT[:, :, :], ps[0:T, 0, 0:256].rearrange("p (r n) -> p r n", r=2), ACT.Copy)\
                    .then_inc(nm_copied, 1)
                with act.Fori(0, THIRDS) as third:
                    with act.Fori(0, T // 2) as i:
                        for k in range(4):
                            at = b * B_UNITS + third * (2 * T) + i * 4 + k
                            act.wait_ge(st_mm, at + 1)
                            act.wait_ge(p_used, at + (1 + B_CREDIT - 4))
                            act.wait_ge(p_summed, at + (1 + B_CREDIT - 4))
                            nc.scalar.activation(p0[:, k, :], unit(k).rearrange("p a n -> p (a n)"), ACT.Exp)\
                                .then_inc(p_exp, 1)
                    act.wait_ge(p_used, b * B_UNITS + third * (2 * T) + (2 * T + B_CREDIT))
                    act.wait_ge(y_done, b * THIRDS + third + 1)
                    nc.scalar.activation(yn[:, bass.ds(third * 2, 2), :], ps[:, 6:8, 0:QW], ACT.Copy)\
                        .then_inc(y_copied, 1)
                    nc.scalar.activation(z_sb[:, :, QD:QW], ps[:, 6:8, QW:2 * QW - QD], ACT.Copy).then_inc(y_copied, 1)
                    act.wait_ge(z_mm, b * THIRDS + third + 2)
                    nc.scalar.activation(z_sb[:, :, 0:QD], ps[:, 6:8, 0:QD], ACT.Copy).then_inc(z_copied, 1)
                project_hi(b, jobs1, len(jobs0))
                def copy_fill(pair, parity, f, early):
                    e = evac_slot(parity, f)
                    n = ACT_FILLS.index(f)
                    act.wait_ge(fill_mm, b * (PAIRS * FILLS) + pair * FILLS + (f + 1))
                    if not (early and n < 2):
                        act.wait_ge(fill_pool, b * (PAIRS * len(ACT_FILLS)) + pair * len(ACT_FILLS) + (n - 1))
                    nc.scalar.activation(evac[:, e, :], ps[:, fill_bank(parity, f), :], ACT.Copy)\
                        .then_inc(fill_copied, 1)

                def step(pair, parity, main, tail):
                    for s in range(STEPS):
                        tile, j = ORDER[s]
                        if main and not tail and s == NJ:
                            act.wait_ge(vT_out, b * 16 + 16)
                            for slot in v_in:
                                act.wait_ge(slot, b * (8 * PAIRS) + 16)
                        act.wait_ge(t_max, b * (PAIRS * STEPS) + pair * STEPS + (s + 1))
                        shared = tile == 1 and j in SHARED
                        if main if shared else tail:
                            act.wait_ge(fill_mm, b * (PAIRS * FILLS) + pair * FILLS
                                        + (LAST_FILL[j] + 1 - (1 if shared else 2) * FILLS))
                        st = stat[:, tile, :]
                        nc.scalar.activation(p1_slot(parity, tile, j),
                                             chunk_scores(s).rearrange("p a n -> p (a n)"),
                                             ACT.Exp, bias=st[:, NM + j:NM + j + 1],
                                             accum_out=st[:, SS + j:SS + j + 1]).then_inc(t_exp, 1)
                        if s % NJ == NJ - 1:
                            act.wait_ge(m_min, b * T + pair * 2 + (tile + 1))
                            nc.scalar.activation(st[:, EE:EE + NJ], st[:, NM:NM + NJ], ACT.Exp,
                                                 bias=st[:, MIN:MIN + 1], scale=-1.0).then_inc(m_exp, 1)
                        for back, hf in half_fills(s, main, tail):
                            if hf % 2 and hf // 2 in ACT_FILLS:
                                copy_fill(pair - back, (parity + back) % 2, hf // 2, back == 1 and not tail)

                pair_steps(act, step)
                for back, hf in FLUSH:
                    if hf % 2 and hf // 2 in ACT_FILLS:
                        copy_fill(PAIRS - back, (PAIRS - back) % 2, hf // 2, False)

        @block.vector
        def _(dve):
            def project_lo(b, jobs, base, hi_base):
                his = 0
                for k, (name, h, c) in enumerate(jobs):
                    if name in "gv":
                        bias, wide, dst, n = (W_BG, D, gT, GT) if name == "g" else (W_BV, 64, vT, VT)
                        dve.wait_ge(proj_mm, b * JOBS + (base + k + 1))
                        nc.vector.tensor_tensor(
                            dst[:, :].rearrange("p (h t d) -> p h t d", h=2, d=wide)[:, :, c:c + n, :],
                            ps[:, k % 8, 0:2 * n * wide].rearrange("p (t h d) -> p h t d", h=2, d=wide),
                            w[:, bias:bias + wide].unsqueeze(1).unsqueeze(1).broadcast_to((128, 2, n, wide)),
                            ALU.add).then_inc(proj_lo, 1)
                        continue
                    his += 1
                    dst, lo, bias = split_target(name, h, c)
                    r = slice(D * lo, D * lo + D)
                    dve.wait_ge(proj_hi, b * HI_JOBS + (hi_base + his))
                    if bias is None:
                        ins = nc.vector.tensor_tensor(dst[r, :], ps[r, k % 8, :], dst[r, :].bitcast(F32), ALU.subtract)
                    else:
                        ins = nc.vector.scalar_tensor_tensor(
                            out=dst[r, :], in0=ps[r, k % 8, :], scalar=w[r, bias:bias + 1],
                            in1=dst[r, :].bitcast(F32), op0=ALU.add, op1=ALU.subtract)
                    ins.then_inc(proj_lo, 1)

            dve.sem_inc(p_summed, B_CREDIT)
            dve.sem_inc(y_done, 1)
            dve.wait_ge(w_in, 16)
            for h in range(2):
                r = slice(64 * h, 64 * h + 64)
                wp = w[r, W_P + h * P3:W_P + (h + 1) * P3]
                for k in range(2):
                    nc.vector.tensor_scalar(w_half[r, k, :], wp, -0.5 if h and k else 0.5, None, ALU.mult)\
                        .then_inc(w_half_done, 1)
            with dve.Fori(0, B) as b:
                project_lo(b, jobs0, 0, 0)
                nc.vector.memset(part[:, 3, :], 0.0).then_inc(nm_tile, 1)

                def tile_maxima(first, n, col, units):
                    dve.wait_ge(s_max, units + A_CREDIT)
                    nc.vector.tensor_reduce(negmax[:, col], part[:, first:first + n, :], AX.X, ALU.max, negate=True)\
                        .then_inc(nm_tile, 1)

                with dve.Fori(0, T // 4) as i:
                    for u in range(4 * AU):
                        at = b * A_UNITS + i * (4 * AU)
                        if u == 0:
                            dve.wait_ge(nm_tile, b * NM_TILE + i * 2 + 1)
                        if u == 3 * AU:
                            dve.wait_ge(nm_tile, b * NM_TILE + i * 2 + 2)
                        dve.wait_ge(s_mm, at + (u + 1))
                        dve.wait_ge(s_abs, at + (u + 1 + A_CREDIT))
                        apart(dve)
                        n = AW[u % AU]
                        d = absd[:, u % AU, :, 0:n]
                        nc.vector.tensor_tensor_reduce(
                            out=d, in0=ps[:, 4 * (u % 2):4 * (u % 2) + 2, 0:n], in1=d, scale=1.0,
                            scalar=-3.0e38, op0=ALU.add, op1=ALU.max,
                            accum_out=part[:, u // AU, u % AU:u % AU + 1]).then_inc(s_max, 1)
                        if u == 0:
                            tile_maxima(3, 1, bass.ds(i * 4, 1), at)
                        if u == 3 * AU:
                            tile_maxima(0, 3, bass.ds(i * 4 + 1, 3), at + 3 * AU)
                tile_maxima(3, 1, slice(T, T + 1), b * A_UNITS + A_UNITS)
                dve.wait_ge(nm_tile, b * NM_TILE + NM_TILE)
                nc.vector.tensor_copy(nmh[:, :], negmax[:, 1:]).then_inc(nm_step, 1)
                dve.wait_ge(nm_step, b * 2 + 1)
                nc.vector.tensor_tensor(nml[:, :], negmax[:, 1:], nmh[:, :].bitcast(F32), ALU.subtract)\
                    .then_inc(nm_step, 1)
                nc.vector.memset(ps[:, 6:8, 0:2 * QW - QD], 0.0).then_inc(o_zero, 1)
                with dve.Fori(0, THIRDS) as third:
                    def sums(i, first):
                        for k in range(4):
                            dve.wait_ge(p_exp, b * B_UNITS + third * (2 * T) + i * 4 + (k + 1))
                            mine = p0[:, k, :].rearrange("p (g q) -> p g q", g=4)[:, :, 0:QD]
                            if first and k < 2:
                                if k == 0:
                                    dve.wait_ge(z_mm, b * THIRDS + third + 1)
                                nc.vector.tensor_copy(psum_p[:, k], mine).then_inc(p_summed, 1)
                                continue
                            dve.wait_ge(p_summed, b * B_UNITS + third * (2 * T) + i * 4 + (k - 1 + B_CREDIT))
                            nc.vector.tensor_tensor(psum_p[:, k % 2], mine, psum_p[:, k % 2], ALU.add)\
                                .then_inc(p_summed, 1)

                    sums(0, True)
                    apart(dve)
                    with dve.Fori(0, T // 2 - 1) as i:
                        sums(i + 1, False)
                    dve.wait_ge(z_copied, b * THIRDS + third + 1)
                    apart(dve)
                    nc.vector.memset(ps[:, 6:8, 0:2 * QW - QD], 0.0).then_inc(o_zero, 1)
                    dve.wait_ge(y_copied, b * (2 * THIRDS) + third * 2 + 2)
                    nc.vector.reciprocal(z_sb[:, :, :], z_sb[:, :, :]).then_inc(z_inv, 1)
                    dve.wait_ge(z_inv, b * THIRDS + third + 1)
                    y = yn[:, bass.ds(third * 2, 2), :]
                    nc.vector.tensor_tensor(y, y, z_sb[:, :, :], ALU.mult).then_inc(y_done, 1)
                    apart(dve)
                for k in range(H // QW):
                    dve.wait_ge(wo_mm, b * (H // QW) + (k + 1))
                    xs = x_sb[:, k * QW:(k + 1) * QW]
                    nc.vector.scalar_tensor_tensor(out=xs, in0=ps[:, k % 8, 0:QW], scalar=w[:, W_BO:W_BO + 1],
                                                   in1=xs, op0=ALU.add, op1=ALU.add).then_inc(x1_done, 1)
                project_lo(b, jobs1, len(jobs0), HI_JOBS0)

                FIRST = BY_DVE[0]

                def add_fill(pair, parity, f, first):
                    dve.wait_ge(fill_mm, b * (PAIRS * FILLS) + pair * FILLS + (f + 1))
                    n = BY_DVE.index(f)
                    if not first:
                        dve.wait_ge(fill_dve, b * (PAIRS * len(BY_DVE)) + pair * len(BY_DVE) + n)
                    xs = x_sb[:, f * BANK:(f + 1) * BANK]
                    nc.vector.tensor_tensor(xs, ps[:, fill_bank(parity, f), :], xs, ALU.add).then_inc(fill_dve, 1)

                def factors(pair, tile, early):
                    st = stat[:, tile, :]
                    dve.wait_ge(m_exp, b * T + pair * 2 + (tile + 1))
                    nc.vector.tensor_tensor_reduce(out=st[:, ES:ES + NJ], in0=st[:, EE:EE + NJ], in1=st[:, SS:SS + NJ],
                                                   scale=1.0, scalar=0.0, op0=ALU.mult, op1=ALU.add,
                                                   accum_out=st[:, SUM:SUM + 1]).then_inc(m_sum, 1)
                    dve.wait_ge(m_sum, b * T + pair * 2 + (tile + 1))
                    nc.vector.reciprocal(st[:, INV:INV + 1], st[:, SUM:SUM + 1]).then_inc(m_inv, 1)
                    dve.wait_ge(m_inv, b * T + pair * 2 + (tile + 1))
                    if not early:
                        dve.wait_ge(vw_done, b * T + pair * 2 + (tile - 1))
                    nc.vector.tensor_scalar(st[:, WW:WW + NJ], st[:, EE:EE + NJ], st[:, INV:INV + 1], None, ALU.mult)\
                        .then_inc(m_fac, 1)

                def step(pair, parity, main, tail):
                    for s in range(STEPS):
                        tile, j = ORDER[s]
                        st = stat[:, tile, :]
                        dve.wait_ge(t_mm, b * (PAIRS * STEPS) + pair * STEPS + (s + 1))
                        nc.vector.tensor_reduce(st[:, NM + j:NM + j + 1], chunk_scores(s)
                                                .rearrange("p a n -> p (a n)"), AX.X, ALU.max, negate=True)\
                            .then_inc(t_max, 1)
                        if s % NJ == NJ - 1:
                            dve.wait_ge(t_max, b * (PAIRS * STEPS) + pair * STEPS + (s + 1))
                            nc.vector.tensor_reduce(st[:, MIN:MIN + 1], st[:, NM:NM + NJ], AX.X, ALU.min)\
                                .then_inc(m_min, 1)
                        if s == 0 and main:
                            factors(pair - 1, 1, not tail)
                        if s == NJ:
                            factors(pair, 0, not main)
                        for back, hf in half_fills(s, main, tail):
                            if hf % 2 and hf // 2 in BY_DVE:
                                add_fill(pair - back, (parity + back) % 2, hf // 2, not tail and hf // 2 == FIRST)

                pair_steps(dve, step)
                factors(PAIRS - 1, 1, False)
                for back, hf in FLUSH:
                    if hf % 2 and hf // 2 in BY_DVE:
                        add_fill(PAIRS - back, (PAIRS - back) % 2, hf // 2, False)

        @block.gpsimd
        def _(pool):
            nc.gpsimd.memset(ident[:, :], 0.0).then_inc(id_zero, 1)
            pool.wait_ge(id_zero, 1)
            nc.gpsimd.affine_select(out=ident[:, :], in_=ident[:, :], compare_op=ALU.not_equal, fill=1.0, base=0,
                                    pattern=[[-1, 128]], channel_multiplier=1).then_inc(const_done, 1)
            nc.gpsimd.memset(ones[:, :], 1.0).then_inc(const_done, 1)
            pool.wait_ge(const_done, 2)
            nc.gpsimd.memset(kslot[:, :, :, :].bitcast(F32), 0.0).then_inc(const_done, 1)
            pool.wait_ge(const_done, 3)
            with pool.Fori(0, B) as b:
                for n, rest in enumerate((psd, thslot, th, ph)):
                    nc.gpsimd.memset(rest[P3:K].bitcast(F32), 0.0).then_inc(rest_zero, 1)
                pool.wait_ge(rest_zero, b * 4 + 4)
                apart(pool)
                nc.gpsimd.memset(ph[P3:P3 + 2, :].bitcast(F32), 1.0).then_inc(ones_set, 1)
                pool.wait_ge(ones_set, b + 1)
                pool.wait_ge(x1_done, b * (H // QW) + H // QW)
                apart(pool)
                nc.gpsimd.memset(qst[P3:K].bitcast(F32), 0.0).then_inc(q_zero, 1)
                pool.wait_ge(q_zero, b + 1)

                FIRST = ACT_FILLS[0]

                def add_fill(pair, parity, f, first):
                    n = ACT_FILLS.index(f)
                    count = b * (PAIRS * len(ACT_FILLS)) + pair * len(ACT_FILLS) + (n + 1)
                    pool.wait_ge(fill_copied, count)
                    if not first:
                        pool.wait_ge(fill_pool, count - 1)
                    xs = x_sb[:, f * BANK:(f + 1) * BANK]
                    nc.gpsimd.tensor_tensor(xs, evac[:, evac_slot(parity, f), :], xs, ALU.add).then_inc(fill_pool, 1)

                def weigh_v(pair, parity, tile):
                    pool.wait_ge(m_fac, b * T + pair * 2 + (tile + 1))
                    pool.wait_ge(v_in[parity], b * (8 * PAIRS) + (pair - parity) * 8 + 16)
                    nc.gpsimd.tensor_tensor(
                        vw[:, 2 * parity + tile],
                        vslot[:, parity, 64 * tile:64 * tile + 64].unsqueeze(1).broadcast_to((128, NJ, 64)),
                        stat[:, tile, WW:WW + NJ].unsqueeze(2).broadcast_to((128, NJ, 64)),
                        ALU.mult).then_inc(vw_done, 1)

                def step(pair, parity, main, tail):
                    for s in range(STEPS):
                        if s == 0 and main:
                            weigh_v(pair - 1, 1 - parity, 1)
                        if s == NJ:
                            weigh_v(pair, parity, 0)
                        for back, hf in half_fills(s, main, tail):
                            if hf % 2 and hf // 2 in ACT_FILLS:
                                add_fill(pair - back, (parity + back) % 2, hf // 2, not tail and hf // 2 == FIRST)

                pair_steps(pool, step)
                weigh_v(PAIRS - 1, (PAIRS - 1) % 2, 1)
                for back, hf in FLUSH:
                    if hf % 2 and hf // 2 in ACT_FILLS:
                        add_fill(PAIRS - back, (PAIRS - back) % 2, hf // 2, False)
                pool.wait_ge(fill_pool, b * (PAIRS * len(ACT_FILLS)) + PAIRS * len(ACT_FILLS))
                apart(pool)


def pack_weights(Wg, bg, Wt, bt, Wp, bp, Wo, bo, Wq, bq, Wk, bk, Wv, bv):
    import numpy as np

    pack = np.zeros((128, W_COLS), np.float32)

    def stack(col, bias_col, W, b):
        for block in range(3):
            for half in range(2):
                at = col + half * P3 + D * block
                pack[64 * half:64 * half + 64, at:at + W.shape[0]] = W.T
            pack[D * block:D * block + W.shape[0], bias_col] = b

    stack(W_T, W_BT, Wt, bt)
    stack(W_P, W_BP, Wp, bp)
    for half in range(2):
        for block in range(3):
            at = D * block + DQ * half
            for col, bias_col, W, b in ((W_Q, W_BQ, Wq, bq), (W_K, W_BK, Wk, bk)):
                pack[64 * half:64 * half + 64, col + at:col + at + DQ] = W.T
                pack[at:at + DQ, bias_col] = b
        rows = slice(64 * half, 64 * half + 64)
        pack[rows, W_G + D * half:W_G + D * half + D] = Wg.T
        pack[rows, W_V + 64 * half:W_V + 64 * half + 64] = Wv.T
        pack[rows, W_BO] = bo
    for group in range(4):
        pack[D * group:D * group + D, W_O + 64 * group:W_O + 64 * group + 64] = Wo.T
    pack[:, W_BG:W_BG + D] = bg
    pack[:, W_BV:W_BV + 64] = bv
    return pack


def kernel(**inputs):
    import numpy as np
    import concourse.bacc as bacc
    from concourse.bass_utils import run_bass_kernel_spmd

    a = {k: np.asarray(v) for k, v in inputs.items()}
    B, C, HH, WWD = a["x"].shape
    arrays = {
        "x": np.ascontiguousarray(a["x"]).reshape(B, C, HH * WWD),
        "wpack": pack_weights(*[a[f"L0_conv_{n}"] for n in ("Wg", "bg", "Wt", "bt", "Wp", "bp", "Wo", "bo")],
                              *[a[f"L1_conv_{n}"] for n in ("Wq", "bq", "Wk", "bk", "Wv", "bv")]),
    }
    nc = bacc.Bacc("TRN2", target_bir_lowering=False, num_devices=1)
    aps = [nc.dram_tensor(n, v.shape, mybir.dt.from_np(v.dtype), kind="ExternalInput").ap() for n, v in arrays.items()]
    out = nc.dram_tensor("out", (B, C, HH * WWD), F32, kind="ExternalOutput").ap()
    attention_kernel(nc, *aps, out)
    r = run_bass_kernel_spmd(nc, [arrays], core_ids=[0])
    return r.results[0]["out"].reshape(B, C, HH, WWD)
```
